# Optimizing a Trainium2 kernel written in Bass

```python
import numpy as np
import jax
import jax.numpy as jnp

def _softmax(x, axis=-1):
    return jax.nn.softmax(x, axis=axis)

def _gelu(x):
    return jax.nn.gelu(x, approximate=True)

def _silu(x):
    return jax.nn.silu(x)

def _sigmoid(x):
    return jax.nn.sigmoid(x)

def _layernorm(x, axis=-1, eps=1e-05):
    m = jnp.mean(x, axis=axis, keepdims=True)
    v = jnp.var(x, axis=axis, keepdims=True)
    return (x - m) / jnp.sqrt(v + eps)

def _scatter_add(tgt, idx, src, axis=0):
    return tgt.at[idx].add(src)

def _segment_sum(src, seg, n):
    return jax.ops.segment_sum(src, seg, n)
kernel_name = 'mk_adj_preln_d4_adj_r2_eebd0e'

def setup_inputs(seed: int=0):
    np.random.seed(seed)
    _w = jnp.asarray

    def _rec_inputs():
        import jax
        import jax.numpy as jnp
        _gk = jax.random.key(seed)
        x = -0.001003 + 1 * jax.random.normal(jax.random.fold_in(_gk, 1), (6144, 128), jnp.float32)
        _a = jax.random.bernoulli(jax.random.fold_in(_gk, 2), 0.000325521, (6144, 6144))
        adj = _a.astype(jnp.int32)
        return (x, adj)
    x, adj = _rec_inputs()

    def _L0_gnn_setup():
        import jax, jax.numpy as jnp
        import numpy as np
        M = 6144
        N = 6144
        D = 128
        TEMPERATURE = 0.07
        NEG_PAD = jnp.float32(-2 ** 32 + 1)
        key = jax.random.key(seed)
        k1, k2, k3, k4 = jax.random.split(key, 4)
        xx_anchor = jax.random.normal(k1, (M, D), dtype=jnp.float32)
        inp = jax.random.normal(k2, (N, D), dtype=jnp.float32)
        adj = (jax.random.uniform(k3, (M, N)) < 0.002).astype(jnp.int32)
        limit = jnp.sqrt(6.0 / (D + D)).astype(jnp.float32)
        weight = jax.random.uniform(k4, (D, D), minval=-limit, maxval=limit, dtype=jnp.float32)
        return {'xx_anchor': xx_anchor, 'input': inp, 'adj': adj, 'weight': weight}
    _L0_gnn_all = _L0_gnn_setup()
    _L0_gnn_in = {k: v for k, v in _L0_gnn_all.items() if k in ('input', 'weight')}
    del _L0_gnn_all

    def _L1_gnn_setup():
        import jax, jax.numpy as jnp
        import numpy as np
        N, D = (4096, 128)
        key = jax.random.key(seed)
        k1, k2, k3 = jax.random.split(key, 3)
        adj = jax.random.randint(k1, (N, N), 0, 2, dtype=jnp.int32)
        emb = jax.random.normal(k2, (N, D), dtype=jnp.float32)
        attn = jax.random.normal(k3, (2 * D, 1), dtype=jnp.float32)
        return {'adj': adj, 'emb': emb, 'attn': attn}
    _L1_gnn_all = _L1_gnn_setup()
    _L1_gnn_in = {k: v for k, v in _L1_gnn_all.items() if k in ('attn',)}
    del _L1_gnn_all

    def _L2_gnn_setup():
        import jax, jax.numpy as jnp
        import numpy as np
        ALPHA = 0.2
        NEG_INF = -9000000000000000.0
        key = jax.random.key(seed)
        k1, k2, k3, k4 = jax.random.split(key, 4)
        N, F_IN, F_OUT = (4096, 128, 128)
        h = jax.random.normal(k1, (N, F_IN), dtype=jnp.float32)
        adj = jax.random.randint(k2, (N, N), 0, 2, dtype=jnp.int32)
        W = jax.random.normal(k3, (F_IN, F_OUT), dtype=jnp.float32) * (1.414 / np.sqrt(F_IN))
        a = jax.random.normal(k4, (2 * F_OUT, 1), dtype=jnp.float32) * (1.414 / np.sqrt(2 * F_OUT))
        return {'h': h, 'adj': adj, 'W': W, 'a': a}
    _L2_gnn_all = _L2_gnn_setup()
    _L2_gnn_in = {k: v for k, v in _L2_gnn_all.items() if k in ('W', 'a')}
    del _L2_gnn_all

    def _L3_gnn_setup():
        import jax, jax.numpy as jnp
        import numpy as np
        N = 4096
        F_IN = 128
        D = 128
        NEG_SLOPE = 0.2
        MASK_FILL = -9000000000000000.0
        key = jax.random.key(seed)
        k1, k2, k3, k4 = jax.random.split(key, 4)
        A = jax.random.randint(k1, (N, N), 0, 2, dtype=jnp.int32)
        X = jax.random.normal(k2, (N, F_IN), dtype=jnp.float32)
        lim_w = float(np.sqrt(6.0 / (F_IN + D)))
        Ws = jax.random.uniform(k3, (F_IN, D), minval=-lim_w, maxval=lim_w, dtype=jnp.float32)
        lim_a = 1.414 * float(np.sqrt(6.0 / (2 * D + 1)))
        a = jax.random.uniform(k4, (2 * D, 1), minval=-lim_a, maxval=lim_a, dtype=jnp.float32)
        return {'A': A, 'X': X, 'Ws': Ws, 'a': a}
    _L3_gnn_all = _L3_gnn_setup()
    _L3_gnn_in = {k: v for k, v in _L3_gnn_all.items() if k in ('Ws', 'a')}
    del _L3_gnn_all
    return {'x': x, 'adj': adj, 'L0_gnn_input': _L0_gnn_in['input'], 'L0_gnn_weight': _L0_gnn_in['weight'], 'L1_gnn_attn': _L1_gnn_in['attn'], 'L2_gnn_W': _L2_gnn_in['W'], 'L2_gnn_a': _L2_gnn_in['a'], 'L3_gnn_Ws': _L3_gnn_in['Ws'], 'L3_gnn_a': _L3_gnn_in['a']}

def reference(x, adj, L0_gnn_input, L0_gnn_weight, L1_gnn_attn, L2_gnn_W, L2_gnn_a, L3_gnn_Ws, L3_gnn_a):
    import jax
    import jax.numpy as jnp

    def _L0_gnn_ref(xx_anchor, input, adj, weight):
        import jax, jax.numpy as jnp
        import numpy as np
        M = 6144
        N = 6144
        D = 128
        TEMPERATURE = 0.07
        NEG_PAD = jnp.float32(-2 ** 32 + 1)
        anchor_adj = jnp.einsum('md,de,ne->mn', xx_anchor, weight, input)
        scores = jnp.where(adj > 0, anchor_adj, NEG_PAD)
        atten = jax.nn.softmax(scores / TEMPERATURE, axis=1)
        return atten @ input

    def _L1_gnn_ref(adj, emb, attn):
        import jax, jax.numpy as jnp
        import numpy as np
        N, D = (4096, 128)
        d = emb.shape[1]
        s_i = emb @ attn[:d]
        s_j = emb @ attn[d:]
        e = jax.nn.leaky_relu(s_i + s_j.T, negative_slope=0.2)
        neg_inf = jnp.float32(-1000000000.0)
        e = e + jnp.where(adj > 0, jnp.float32(0.0), neg_inf)
        alpha = jax.nn.softmax(e, axis=1)
        return alpha @ emb

    def _L2_gnn_ref(h, adj, W, a):
        import jax, jax.numpy as jnp
        import numpy as np
        ALPHA = 0.2
        NEG_INF = -9000000000000000.0
        Wh = h @ W
        F_out = W.shape[1]
        e_src = Wh @ a[:F_out, 0]
        e_dst = Wh @ a[F_out:, 0]
        e = jax.nn.leaky_relu(e_src[:, None] + e_dst[None, :], negative_slope=ALPHA)
        attention = jax.nn.softmax(jnp.where(adj > 0, e, NEG_INF), axis=1)
        h_prime = attention @ Wh
        return h_prime

    def _L3_gnn_ref(A, X, Ws, a):
        import jax, jax.numpy as jnp
        import numpy as np
        N = 4096
        F_IN = 128
        D = 128
        NEG_SLOPE = 0.2
        MASK_FILL = -9000000000000000.0
        Wh = X @ Ws
        d = Wh.shape[-1]
        e1 = Wh @ a[:d]
        e2 = Wh @ a[d:]
        e = jax.nn.leaky_relu(e1 + e2.T, negative_slope=NEG_SLOPE)
        e = jnp.where(A > 0, e, MASK_FILL)
        attn = jax.nn.softmax(e, axis=1)
        H = attn @ Wh
        return H
    h = jnp.maximum(_layernorm(x, axis=-1), 0.0)
    x = x + _L0_gnn_ref(h, L0_gnn_input, adj, L0_gnn_weight)
    h = jnp.maximum(_layernorm(x, axis=-1), 0.0)
    x = x + _L1_gnn_ref(adj, h, L1_gnn_attn)
    h = jnp.maximum(_layernorm(x, axis=-1), 0.0)
    x = x + _L2_gnn_ref(h, adj, L2_gnn_W, L2_gnn_a)
    h = jnp.maximum(_layernorm(x, axis=-1), 0.0)
    x = x + _L3_gnn_ref(adj, h, L3_gnn_Ws, L3_gnn_a)
    return x

_drawn_inputs = setup_inputs


def setup_inputs(seed=0):
    import zlib

    import numpy as np

    out = dict(_drawn_inputs(seed))
    spreads = {}
    factors = {}
    for name, (base, spread) in spreads.items():
        noise = np.random.default_rng([zlib.crc32(name.encode()), seed]).standard_normal(out[name].shape)
        drawn = base * np.exp(spread * noise) if base else spread * noise
        out[name] = jnp.asarray(drawn.astype(out[name].dtype))
    for name, factor in factors.items():
        out[name] = (out[name] * factor).astype(out[name].dtype)
    return out
```

```python
import concourse.bass as bass
from concourse import mybir
from contextlib import ExitStack

F32, I32, U32, BF16 = mybir.dt.float32, mybir.dt.int32, mybir.dt.uint32, mybir.dt.bfloat16
ALU, ACT, AX = mybir.AluOpType, mybir.ActivationFunctionType, mybir.AxisListType

P = 128
N = 6144
D = 128
T = N // P
BANK = 512
CH = N // BANK
TPC = BANK // P
LAYERS = 4
SLOPE = 0.2
EPS = 1e-5
PENALTY = [-1e30, -1e9, -9e15, -9e15]
SCALE = [1.0 / 0.07, 1.0, 1.0, 1.0]


def general_path(nc, r, adj_d, x_d, inp_d, out_d):
    X, H, HT, VAL, COL, ADJ, PEN = r.region
    E, QT, PT = HT, H, PEN
    x3 = lambda b: b[:, :].rearrange("p (t d) -> p t d", d=D)
    adj_v = adj_d.rearrange("(p t) j -> p t j", t=T)
    row_major = lambda d: d.rearrange("(p t) d -> p t d", t=T)
    g = r.general

    def values(L):
        return x3(H) if L == 1 else x3(VAL)

    def sp(eng):
        eng.dma_start(x3(X), row_major(x_d)).then_inc(g["x_loaded"], 16)
        eng.dma_start(x3(VAL), row_major(inp_d)).then_inc(g["x_loaded"], 16)
        for L in range(LAYERS):
            with eng.Fori(0, T) as t:
                eng.wait_ge(g["penalty_ready"], t + (L * T + 1))
                eng.dma_start(ADJ[:, :].rearrange("p (o j) -> p o j", o=1).bitcast(I32),
                              adj_v[:, bass.ds(t, 1), :]).then_inc(g["adj_loaded"], 16)
        eng.wait_ge(g["row_done"], LAYERS * T)
        eng.dma_start(row_major(out_d), x3(X)).then_inc(g["stored"], 16)
        eng.wait_ge(g["stored"], 16)

    def vector(eng):
        n = [0]

        def link(ins):
            n[0] += 1
            ins.then_inc(g["vector_step"], 1)
            eng.wait_ge(g["vector_step"], n[0])

        nc.vector.memset(r.scrap[:], 0.0).then_inc(g["penalty_ready"], 1)
        eng.wait_ge(g["x_loaded"], 32)
        evac = 0
        for L in range(LAYERS):
            h = x3(H)
            if L:
                eng.wait_ge(g["row_done"], L * T)
            link(nc.vector.reduce_sum(r.mean[:], x3(X), AX.X))
            link(nc.vector.tensor_scalar(r.mean[:], r.mean[:], 1.0 / D, None, ALU.mult))
            link(nc.vector.tensor_tensor(h, x3(X), r.mean[:].unsqueeze(2).to_broadcast((P, T, D)), ALU.subtract))
            link(nc.vector.tensor_tensor(x3(PEN), h, h, ALU.mult))
            nc.vector.reduce_sum(r.var[:], x3(PEN), AX.X).then_inc(g["var_ready"], 1)
            eng.wait_ge(g["std_ready"], L + 1)
            link(nc.vector.reciprocal(r.rstd[:], r.std[:]))
            nc.vector.scalar_tensor_tensor(out=h, in0=h, scalar=0.0, in1=r.rstd[:].unsqueeze(2).to_broadcast((P, T, D)),
                                           op0=ALU.max, op1=ALU.mult).then_inc(g["h_ready"], 1)
            for c in range(CH):
                eng.wait_ge(g["psum_filled"], evac + 1)
                nc.vector.tensor_copy(HT[:, c * BANK:(c + 1) * BANK], r.ps[c % 4][:, :]).then_inc(g["psum_emptied"], 1)
                evac += 1
            if L == 0:
                for dst in (QT, COL):
                    for c in range(CH):
                        eng.wait_ge(g["psum_filled"], evac + 1)
                        nc.vector.tensor_copy(dst[:, c * BANK:(c + 1) * BANK], r.ps[c % 4][:, :]).then_inc(g["psum_emptied"], 1)
                        evac += 1
            else:
                for t in range(T):
                    eng.wait_ge(g["psum_filled"], evac + 1)
                    if L > 1:
                        nc.vector.tensor_copy(x3(VAL)[:, t, :], r.ps[t % 4][:, 0:D])
                    nc.vector.tensor_copy(r.score[:, t, :], r.ps[t % 4][:, D:D + 2]).then_inc(g["psum_emptied"], 1)
                    evac += 1
                for c in range(CH):
                    eng.wait_ge(g["psum_filled"], evac + 1)
                    nc.vector.tensor_copy(COL[:, c * BANK:(c + 1) * BANK], r.ps[c % 4][:, :]).then_inc(g["psum_emptied"], 1)
                    evac += 1
            link(nc.vector.memset(r.scrap[:], 0.0))
            if L:
                eng.wait_ge(g["psum_emptied"], evac)
            per = 6 if L else 4
            base = n[0]
            with eng.Fori(0, T) as t:
                k = [0]

                def step(ins):
                    k[0] += 1
                    ins.then_inc(g["vector_step"], 1)
                    eng.wait_ge(g["vector_step"], t * per + (base + k[0]))

                eng.wait_ge(g["adj_loaded"], t * 16 + 16 * (L * T + 1))
                nc.vector.tensor_scalar(PEN[:, :], ADJ[:, :].bitcast(I32), 0.0, PENALTY[L], ALU.is_le, ALU.mult).then_inc(g["penalty_ready"], 1)
                if L == 0:
                    nc.vector.tensor_copy(r.query[:], QT[:, bass.ds(t * P, P)]).then_inc(g["query_ready"], 1)
                eng.wait_ge(g["penalty_ready"], t + (L * T + 2))
                if L:
                    step(nc.vector.tensor_scalar(E[:, :], COL[:, :], r.score[:, bass.ds(t, 1), 0], None, ALU.add))
                    step(nc.vector.scalar_tensor_tensor(out=E[:, :], in0=E[:, :], scalar=SLOPE, in1=E[:, :], op0=ALU.mult, op1=ALU.max))
                else:
                    eng.wait_ge(g["scores_ready"], t * CH + CH)
                step(nc.vector.tensor_tensor(E[:, :].rearrange("i (t p) -> i t p", t=T), E[:, :].rearrange("i (t p) -> i t p", t=T),
                                             PEN[:, :].rearrange("i (p t) -> i t p", t=T), ALU.add))
                step(nc.vector.reduce_max(r.rowmax[:], E[:, :], AX.X))
                nc.vector.tensor_scalar(E[:, :], E[:, :], r.rowmax[:, 0:1], SCALE[L], ALU.subtract, ALU.mult).then_inc(g["masked"], 1)
                eng.wait_ge(g["aggregated"], t + (L * T + 1))
                step(nc.vector.reciprocal(r.rz[:], r.z[:]))
                step(nc.vector.tensor_scalar(r.agg[:], r.ps[4][:, 0:D], r.rz[:, 0:1], None, ALU.mult))
                xt = x3(X)[:, bass.ds(t, 1), :]
                nc.vector.tensor_tensor(xt, xt, r.agg[:].rearrange("p (o d) -> p o d", o=1), ALU.add).then_inc(g["row_done"], 1)
                assert k[0] == per
            n[0] = base + T * per

    def scalar(eng):
        eng.wait_ge(r.eps_ready, 1)
        for L in range(LAYERS):
            eng.wait_ge(g["var_ready"], L + 1)
            nc.scalar.activation(r.std[:], r.var[:], ACT.Sqrt, bias=r.eps[:, 0:1], scale=1.0 / D).then_inc(g["std_ready"], 1)
            with eng.Fori(0, T) as t:
                if L == 0:
                    for c in range(CH):
                        eng.wait_ge(g["score_filled"], t * CH + (c + 1))
                        nc.scalar.copy(E[:, c * BANK:(c + 1) * BANK], r.ps[c % 4][:, :]).then_inc(g["scores_ready"], 1)
                eng.wait_ge(g["masked"], t + (L * T + 1))
                nc.scalar.activation(E[:, :], E[:, :], ACT.Exp, accum_out=r.z[:, 0:1]).then_inc(g["probs_ready"], 1)
                for c in range(CH):
                    eng.wait_ge(g["probs_turned"], t * CH + (L * T * CH + c + 1))
                    nc.scalar.copy(PT[:, c * BANK:(c + 1) * BANK], r.ps[c % 4][:, :]).then_inc(g["turned_copied"], 1)

    def tensor(eng):
        eng.wait_ge(r.weights_ready, r.WEIGHTS_READY)
        filled = 0

        def fill(bank_free):
            if bank_free > 4:
                eng.wait_ge(g["psum_emptied"], bank_free - 4)

        for L in range(LAYERS):
            eng.wait_ge(g["h_ready"], L + 1)
            if L:
                eng.wait_ge(g["turned_copied"], L * T * CH)
            for c in range(CH):
                fill(filled + 1)
                for q in range(TPC):
                    t = c * TPC + q
                    last = nc.tensor.transpose(r.ps[c % 4][:, q * P:(q + 1) * P], x3(H)[:, t, :], r.ident[:])
                last.then_inc(g["psum_filled"], 1)
                filled += 1
            eng.wait_ge(g["psum_emptied"], filled)
            if L == 0:
                for c in range(CH):
                    fill(filled + 1)
                    nc.tensor.matmul(r.ps[c % 4][:, :], r.w0[:], HT[:, c * BANK:(c + 1) * BANK], start=True, stop=True).then_inc(g["psum_filled"], 1)
                    filled += 1
                for c in range(CH):
                    fill(filled + 1)
                    for q in range(TPC):
                        last = nc.tensor.transpose(r.ps[c % 4][:, q * P:(q + 1) * P], x3(VAL)[:, c * TPC + q, :], r.ident[:])
                    last.then_inc(g["psum_filled"], 1)
                    filled += 1
            else:
                for t in range(T):
                    fill(filled + 1)
                    lo = D if L == 1 else 0
                    nc.tensor.matmul(r.ps[t % 4][:, lo:D + 2], HT[:, t * P:(t + 1) * P], r.wext[L][:, lo:D + 2], start=True, stop=True).then_inc(g["psum_filled"], 1)
                    filled += 1
                for c in range(CH):
                    fill(filled + 1)
                    nc.tensor.matmul(r.ps[c % 4][:, :], r.target_rep[L][:], HT[:, c * BANK:(c + 1) * BANK], start=True, stop=True).then_inc(g["psum_filled"], 1)
                    filled += 1
            eng.wait_ge(g["psum_emptied"], filled)
            with eng.Fori(0, T) as t:
                if L == 0:
                    eng.wait_ge(g["query_ready"], t + 1)
                    for c in range(CH):
                        if c >= 4:
                            eng.wait_ge(g["scores_ready"], t * CH + (c - 3))
                        nc.tensor.matmul(r.ps[c % 4][:, :], r.query[:], COL[:, c * BANK:(c + 1) * BANK], start=True, stop=True).then_inc(g["score_filled"], 1)
                eng.wait_ge(g["probs_ready"], t + (L * T + 1))
                for c in range(CH):
                    if c >= 4:
                        eng.wait_ge(g["turned_copied"], t * CH + (L * T * CH + c - 3))
                    for q in range(TPC):
                        b = c * TPC + q
                        last = nc.tensor.transpose(r.ps[c % 4][:, q * P:(q + 1) * P], E[:, b * P:(b + 1) * P], r.ident[:])
                    last.then_inc(g["probs_turned"], 1)
                eng.wait_ge(g["turned_copied"], t * CH + (L * T * CH + CH))
                for b in range(T):
                    last = nc.tensor.matmul(r.ps[4][:, 0:D], PT[:, b * P:(b + 1) * P], values(L)[:, b, :], start=(b == 0), stop=(b == T - 1))
                last.then_inc(g["aggregated"], 1)

    return sp, vector, scalar, tensor
ARENA = 7 * N + 840

SEG = 3
SW = N // SEG
FOUND = 8
SLOTS = 12
SLOT_TILES = [43, 30, 17, 8, 4, 2] + [1] * (SLOTS - 6)
ZERO_T = 40
ZT = T - ZERO_T
CLASSES = 8
REC = 272
REC_Q, REC_NB, REC_ID = D, 2 * D, 2 * D + SLOTS
ROW = D + 2
ROW0 = D + 1
CHUNKS = [(0, 1, 12), (1, 1, 6), (2, 2, 5), (4, 4, 4), (8, 5, 3), (13, 4, 3), (17, 7, 2), (24, 6, 2), (30, 5, 1), (35, 5, 1), (40, 4, 1), (44, 4, 0)]
NC = len(CHUNKS)
RING = 3
CAP = 20
GROUP = 3


def chunk_tiles(c):
    t0, n, k = CHUNKS[c]
    return [t for t in range(t0, t0 + n) if t < SLOT_TILES[0]]


def chunk_groups(c):
    t0, n, k = CHUNKS[c]
    return [list(range(t, min(t + GROUP, t0 + n))) for t in range(t0, t0 + n, GROUP)]


ORDER = [[8, 9, 7, 10, 11, 6, 5, 4, 3, 2, 1, 0], [8, 9, 7, 6, 5, 4, 3, 2, 10, 11, 1, 0]] + 2 * [[8, 9, 7, 10, 11, 6, 5, 4, 3, 2, 1, 0]]
FIRST_T = 30
NG = sum(len(chunk_groups(c)) for c in range(NC))
GATHERS = [len(chunk_tiles(c)) * CHUNKS[c][2] for c in range(NC)]


DENSE_FIRST = 3


def stage_order(s):
    return ORDER[s - 1]


def groups_before(s, n):
    return sum(len(chunk_groups(c)) for c in stage_order(s)[:n])


DENSE = [list(range(n * T // (NC - 4), (n + 1) * T // (NC - 4))) for n in range(NC - 4)] + 4 * [[]]


def fast_path(nc, r, adj_d, x_d, inp_d, out_d, rec_d, tab_d):
    f = r.fast
    A = r.arena
    at = [0]

    def take(start, size):
        assert start + size <= ARENA, (start, size)
        return A[:, start:start + size]

    adjb = [take(i * N, N).bitcast(I32) for i in range(3)]
    mask_w = SEG * (SW + FOUND) // 2
    mask = [take(3 * N + i * mask_w, mask_w).bitcast(BF16).rearrange("p (s w) -> p s w", s=SEG) for i in range(2)]
    o = 3 * N + 2 * mask_w
    rec = take(o, T * REC).rearrange("p (t c) -> p t c", t=T)
    o_inp = o + T * REC
    inp = take(o_inp, T * ROW0).rearrange("p (t c) -> p t c", t=T)
    recp = take(0, T * REC).rearrange("p (t c) -> p t c", t=T)
    xp = recp[:, :, 0:D]
    o = T * REC
    v_even1 = take(o, T * (ROW + 1)).rearrange("p (t c) -> p t c", t=T)
    o += T * (ROW + 1)
    v_odd1 = take(o, T * (ROW + 1)).rearrange("p (t c) -> p t c", t=T)
    o += T * (ROW + 1)
    v_even, v_odd = v_even1[:, :, 1:], v_odd1[:, :, 1:]
    gat = [take(o + i * CAP * ROW, CAP * ROW) for i in range(RING)]
    o += RING * CAP * ROW
    hb = [take(o + i * GROUP * D, GROUP * D).rearrange("p (t c) -> p t c", t=GROUP) for i in range(2)]
    o += 2 * GROUP * D
    htb = [take(o + i * GROUP * D, GROUP * D) for i in range(2)]
    o += 2 * GROUP * D
    prod = take(o, CAP * D)
    assert o + CAP * D <= o_inp
    ZW = ZT * P
    DB = 4
    s_row, m_row, *db = [take(o_inp + i * ZW, ZW) for i in range(DB + 2)]
    vals = [None, v_odd, v_even, v_odd]
    row_major = lambda d: d.rearrange("(p t) d -> p t d", t=T)
    adj_v = adj_d.rearrange("(p t) j -> p t j", t=T)

    def dense_out(t):
        q = t - ZERO_T
        return r.ps[4 + q // 3][:, q % 3 * (D + 1):(q % 3 + 1) * (D + 1)]

    def sp(eng):
        eng.dma_start(rec[:, :, 0:D], row_major(x_d)).then_inc(f["x_loaded"], 16)
        for t in range(3):
            eng.dma_start(adjb[t].rearrange("p (o j) -> p o j", o=1), adj_v[:, t:t + 1, :]).then_inc(f["adj_loaded%d" % t], 16)
        eng.dma_start(inp[:, :, 0:D], row_major(inp_d)).then_inc(f["inp_loaded"], 16)
        with eng.Fori(0, T // 3 - 1) as i:
            for b in range(3):
                eng.wait_ge(f["mask_made"], i * (3 * SEG) + (b + 1) * SEG)
                eng.dma_start(adjb[b].rearrange("p (o j) -> p o j", o=1),
                              adj_v[:, bass.ds(i * 3 + (b + 3), 1), :]).then_inc(f["adj_loaded%d" % b], 16)
        eng.wait_ge(f["place_ready"], 1)
        eng.dma_start(row_major(tab_d[0]), inp).then_inc(f["table0_written"], 16)
        eng.wait_ge(f["rec_scattered"], 16 * T)
        for i, (lo, hi) in enumerate(((FIRST_T, T), (0, FIRST_T))):
            eng.dma_start(recp[:, lo:hi, :], row_major(rec_d)[:, lo:hi, :]).then_inc(f["rec_loaded%d" % i], 16)
        for s in (1, 2, 3):
            for i, c in enumerate(stage_order(s)):
                t0, n, k = CHUNKS[c]
                eng.wait_ge(f["projected_copied"], (s - 1) * NG + groups_before(s, i + 1))
                eng.dma_start(row_major(tab_d[s])[:, t0:t0 + n, :], vals[s][:, t0:t0 + n, :]).then_inc(f["table_written"], 16)

    def gpsimd(eng):
        nc.gpsimd.iota(r.own_id[:], pattern=[[1, T]], base=0, channel_multiplier=T).then_inc(f["id_ready"], 1)
        eng.memset(r.tri[:], 1.0).then_inc(f["pool_step"], 1)
        eng.wait_ge(f["pool_step"], 1)
        eng.affine_select(out=r.tri[:], in_=r.tri[:], compare_op=ALU.is_gt, fill=0.0, base=0,
                          pattern=[[1, P]], channel_multiplier=-1).then_inc(f["tri_ready"], 1)
        eng.wait_ge(f["place_ready"], 1)
        for t in range(T):
            nc.gpsimd.indirect_dma_start(out=rec_d[:, :], out_offset=bass.IndirectOffsetOnAxis(ap=r.place[:, t:t + 1], axis=0),
                                         in_=rec[:, t, :], in_offset=None).then_inc(f["rec_scattered"], 16)
        for L in range(LAYERS):
            if L == 0:
                eng.wait_ge(f["index_ready"], 1)
                eng.wait_ge(f["table0_written"], 16)
            else:
                eng.wait_ge(f["places_ready"], NC - 1)
                eng.wait_ge(f["table_written"], 16 * NC * L)
            width = ROW if L else ROW0
            index = r.index if L else r.index0
            for n, c in enumerate(ORDER[L]):
                k = CHUNKS[c][2]
                g = L * NC + n
                if L == 0 and CHUNKS[c][0] < FIRST_T:
                    eng.wait_ge(f["index_ready"], 2)
                if g >= RING:
                    eng.wait_ge(f["chunk_done"], g - RING + 1)
                for i, t in enumerate(chunk_tiles(c)):
                    for s in range(k):
                        w = (i * k + s) * width
                        nc.gpsimd.indirect_dma_start(out=gat[g % RING][:, w:w + width], out_offset=None, in_=tab_d[L][:, :],
                                                     in_offset=bass.IndirectOffsetOnAxis(ap=index[:, t, s:s + 1], axis=0)
                                                     ).then_inc(f["gathered%d" % (g % RING)], 16)
                if L == LAYERS - 1 and n >= 2:
                    store(eng, n - 2)
        for n in (NC - 2, NC - 1):
            store(eng, n)
        eng.wait_ge(f["stored"], 16 * T)

    def store(eng, n):
        eng.wait_ge(f["chunk_done"], (LAYERS - 1) * NC + n + 1)
        c = ORDER[LAYERS - 1][n]
        for t in range(CHUNKS[c][0], CHUNKS[c][0] + CHUNKS[c][1]):
            nc.gpsimd.indirect_dma_start(out=out_d[:, :], out_offset=bass.IndirectOffsetOnAxis(ap=r.own_p[:, t:t + 1], axis=0),
                                         in_=xp[:, t, :], in_offset=None).then_inc(f["stored"], 16)

    def vector(eng):
        n = [0]

        def link(ins):
            n[0] += 1
            ins.then_inc(f["vector_step"], 1)
            eng.wait_ge(f["vector_step"], n[0])

        V = nc.vector
        V.memset(r.minus_half[:], -0.5)
        V.memset(r.ones_needle[:], 1.0)
        V.memset(r.ones[:], 1.0)
        V.memset(r.zeros[:], 0.0)
        for s in range(SEG):
            last = V.memset(r.seg_base[:, s * FOUND:(s + 1) * FOUND], float(s * SW + 1))
        link(last)
        for b in range(2):
            V.memset(mask[b][:, :, SW:], 1.0).then_inc(f["mask_free"], 1)
        eng.wait_ge(f["x_loaded"], 16)
        for t in range(T):
            last = V.bn_stats(r.bn[:, t, :], rec[:, t, 0:D])
        link(last)
        for t in range(T):
            last = V.bn_aggr(r.mv[:, t, :], r.bn[:, t, :])
        last.then_inc(f["x_stats_ready"], 1)
        eng.wait_ge(f["x_std_ready"], 1)
        link(V.reciprocal(r.rstd[:], r.std[:]))
        V.scalar_tensor_tensor(out=r.shift[:], in0=r.mv[:, :, 0], scalar=-1.0, in1=r.rstd[:], op0=ALU.mult, op1=ALU.mult).then_inc(f["x_norm_ready"], 1)
        with eng.Fori(0, T // 2) as i:
            for b in range(2):
                eng.wait_ge(f["mask_made"], i * (2 * SEG) + (b + 1) * SEG)
                V.memset(r.scrap[:], 0.0)
                eng.sem_clear(f["search_step"])
                k = [0]

                def step(ins, w=1):
                    k[0] += w
                    ins.then_inc(f["search_step"], w)
                    eng.wait_ge(f["search_step"], k[0])

                for s in range(SEG):
                    last = V.max_index(r.found[:, s * FOUND:(s + 1) * FOUND], r.ones_needle[:], mask[b][:, s, :])
                step(last)
                V.tensor_tensor(r.number[:], r.found[:], r.seg_base[:], ALU.add).then_inc(f["mask_free"], 1)
                eng.wait_ge(f["mask_free"], i * 2 + (b + 3))
                step(V.scalar_tensor_tensor(out=r.number[:], in0=r.found[:], scalar=float(SW), in1=r.number[:], op0=ALU.is_lt, op1=ALU.mult))
                step(V.max(out=r.best[:, 0:8], in_=r.number[:]))
                step(V.match_replace(out=r.number2[:], in_to_replace=r.best[:, 0:8], in_values=r.number[:], imm_value=0.0))
                step(V.max(out=r.best[:, 8:16], in_=r.number2[:]))
                step(V.tensor_copy(rec[:, bass.ds(i * 2 + b, 1), REC_NB:REC_NB + SLOTS], r.best[:, 0:SLOTS].rearrange("p (o k) -> p o k", o=1)))
        eng.wait_ge(f["mask_made"], T * SEG)
        eng.wait_ge(f["id_ready"], 1)
        V.tensor_copy(rec[:, :, REC_ID], r.own_id[:])
        link(V.memset(rec[:, :, REC_ID + 1:REC], 0.0))
        link(V.reduce_sum(r.deg[:], r.cnt[:], AX.X))
        link(V.tensor_scalar(r.deg[:], r.deg[:], float(N), 0.5, ALU.add, ALU.mult))
        for i in range(CLASSES):
            deg = CLASSES - 1 - i
            last = V.tensor_scalar(r.ind[:, i, :], r.deg[:], float(deg), None, ALU.is_ge if i == 0 else ALU.is_equal)
        link(last)
        link(V.tensor_scalar(r.cnt[:], r.cnt[:], float(2 * FOUND - SW), None, ALU.is_gt))
        link(V.tensor_reduce(r.bad2[:, 0:1], r.cnt[:], AX.XY, ALU.max))
        link(V.tensor_scalar(r.deg[:], r.deg[:], float(SLOTS), None, ALU.is_gt))
        link(V.reduce_max(r.bad2[:, 1:2], r.deg[:], AX.X))
        link(V.tensor_tensor(r.bad[:], r.bad2[:, 0:1], r.bad2[:, 1:2], ALU.add))
        V.memset(r.scrap[:], 0.0).then_inc(f["classes_ready"], 1)
        eng.wait_ge(f["ranks_ready"], 1)
        ind = r.ind[:, :, :].rearrange("p c t -> p (c t)")
        CT = CLASSES * T
        link(V.tensor_copy(r.tot[:], r.ps[1][:, 0:CT]))
        link(V.tensor_tensor_scan(out=r.cum[:], data0=r.onesrow[:], data1=r.tot[:], initial=0.0, op0=ALU.mult, op1=ALU.add))
        cum_end = r.cum[:, :].rearrange("p (c t) -> p c t", t=T)[:, :, T - 1]
        link(V.tensor_tensor(r.over[:, 0:CLASSES - 1], cum_end[:, 0:CLASSES - 1], r.caps[:, 0:CLASSES - 1], ALU.is_gt))
        link(V.tensor_scalar(r.over[:, CLASSES - 1:CLASSES], cum_end[:, CLASSES - 2:CLASSES - 1], float(ZERO_T * P), None, ALU.is_lt))
        link(V.reduce_sum(r.bad2[:, 0:1], r.over[:], AX.X))
        link(V.tensor_tensor(r.bad2[:, 1:2], r.bad2[:, 0:1], r.ps[0][:, CT:CT + 1], ALU.add))
        V.tensor_copy(r.flag[:], r.bad2[:, 1:2]).then_inc(f["flag_ready"], 1)
        link(V.tensor_tensor(r.cum[:], r.cum[:], r.tot[:], ALU.subtract))
        link(V.tensor_tensor(r.cum[:], r.cum[:], r.ps[0][:, 0:CT], ALU.add))
        link(V.tensor_tensor(r.cum[:], r.cum[:], ind, ALU.mult))
        link(V.reduce_sum(r.posf[:], r.cum[:, :].rearrange("p (c t) -> p t c", t=T), AX.X))
        link(V.tensor_copy(r.posi[:], r.posf[:]))
        link(V.tensor_scalar(r.low[:], r.posi[:], P - 1, None, ALU.bitwise_and))
        link(V.tensor_scalar(r.high[:], r.posi[:], 7, None, ALU.arith_shift_right))
        V.tensor_copy(r.lowf[:], r.low[:])
        link(V.tensor_copy(r.highf[:], r.high[:]))
        eng.wait_ge(f["inp_loaded"], 16)
        eng.wait_ge(f["x_query_ready"], T)
        link(V.scalar_tensor_tensor(out=inp[:, :, D], in0=r.lowf[:], scalar=float(T), in1=r.highf[:], op0=ALU.mult, op1=ALU.add))
        V.tensor_copy(r.place[:], inp[:, :, D]).then_inc(f["place_ready"], 1)
        for i, (lo, hi) in enumerate(((FIRST_T, T), (0, FIRST_T))):
            eng.wait_ge(f["rec_loaded%d" % i], 16)
            nb = recp[:, lo:hi, REC_NB:REC_NB + SLOTS]
            V.tensor_scalar(r.index0[:, lo:hi, :], nb, -1.0, 0.0, ALU.add, ALU.max).then_inc(f["index_ready"], 1)
            V.tensor_copy(r.own_p[:, lo:hi], recp[:, lo:hi, REC_ID])
            V.tensor_scalar(r.pen[:, lo:hi, :], nb, 0.0, -1e30, ALU.is_le, ALU.mult)
            V.tensor_scalar(r.has[:, lo:hi], recp[:, lo:hi, REC_NB], 0.0, None, ALU.is_gt)
            link(V.tensor_scalar(r.empty[:, lo:hi], recp[:, lo:hi, REC_NB], 0.0, None, ALU.is_le))
        V.memset(v_odd1[:, :, 0:1], 1.0)

        def stats(c):
            t0, m, k = CHUNKS[c]
            for t in range(t0, t0 + m):
                last = V.bn_stats(r.bn[:, t, :], xp[:, t, :])
            link(last)
            for t in range(t0, t0 + m):
                last = V.bn_aggr(r.mv[:, t, :], r.bn[:, t, :])
            last.then_inc(f["stats_ready"], 1)

        def finish_norm(s, n_):
            t0, m, k = CHUNKS[stage_order(s)[n_]]
            eng.wait_ge(f["std_ready"], (s - 1) * NC + n_ + 1)
            link(V.reciprocal(r.rstd[:, t0:t0 + m], r.std[:, t0:t0 + m]))
            V.scalar_tensor_tensor(out=r.shift[:, t0:t0 + m], in0=r.mv[:, t0:t0 + m, 0], scalar=-1.0, in1=r.rstd[:, t0:t0 + m],
                                   op0=ALU.mult, op1=ALU.mult).then_inc(f["norm_ready"], 1)

        arrived = [0] * RING

        def chunk_scores(L, at_):
            c = ORDER[L][at_]
            t0, m, k = CHUNKS[c]
            m = len(chunk_tiles(c))
            g = L * NC + at_
            if not k:
                return
            arrived[g % RING] += 16 * GATHERS[c]
            w = ROW if L else ROW0
            rows = gat[g % RING][:, 0:m * k * w].rearrange("p (t k w) -> p t k w", t=m, k=k)
            e = r.e[g % 2][:, 0:m * k].rearrange("p (t k) -> p t k", k=k)
            eng.wait_ge(f["gathered%d" % (g % RING)], arrived[g % RING])
            if L == 0:
                q = recp[:, t0:t0 + m, REC_Q:REC_Q + D].unsqueeze(2).to_broadcast((P, m, k, D))
                pr = prod[:, 0:m * k * D].rearrange("p (t k d) -> p t k d", t=m, k=k)
                link(V.tensor_tensor(pr, rows[:, :, :, 0:D], q, ALU.mult))
                V.tensor_copy(r.index[:, t0:t0 + m, 0:k], rows[:, :, :, D]).then_inc(f["places_ready"], 1)
                link(V.reduce_sum(e, pr, AX.X))
            else:
                link(V.tensor_tensor(e, rows[:, :, :, D + 1], vals[L][:, t0:t0 + m, D].unsqueeze(2).to_broadcast((P, m, k)), ALU.add))
                link(V.scalar_tensor_tensor(out=e, in0=e, scalar=SLOPE, in1=e, op0=ALU.mult, op1=ALU.max))
            link(V.tensor_tensor(e, e, r.pen[:, t0:t0 + m, 0:k], ALU.add))
            mx = r.mx[:, 0:m]
            link(V.reduce_max(mx, e, AX.X))
            V.tensor_tensor(e, e, mx.unsqueeze(2).to_broadcast((P, m, k)), ALU.subtract).then_inc(f["scores_ready"], 1)

        def chunk_sum(L, at_):
            c = ORDER[L][at_]
            t0, m, k = CHUNKS[c]
            if k:
                neighbour_sum(L, c, L * NC + at_)
            if c >= NC - 2:
                no_neighbours(L, range(t0, t0 + m))

        def neighbour_sum(L, c, g):
            t0, m, k = CHUNKS[c]
            m = len(chunk_tiles(c))
            w = ROW if L else ROW0
            rows = gat[g % RING][:, 0:m * k * w].rearrange("p (t k w) -> p t k w", t=m, k=k)
            ef = r.e[g % 2]
            e = ef[:, 0:m * k].rearrange("p (t k) -> p t k", k=k)
            scored[0] += 1
            eng.wait_ge(f["exp_ready"], scored[0])
            link(V.reduce_sum(r.mx[:, 0:m], e, AX.X))
            link(V.reciprocal(r.mx[:, 0:m], r.mx[:, 0:m]))
            if t0 + m > ZERO_T:
                link(V.tensor_tensor(r.mx[:, 0:m], r.mx[:, 0:m], r.has[:, t0:t0 + m], ALU.mult))
            link(V.tensor_tensor(e, e, r.mx[:, 0:m].unsqueeze(2).to_broadcast((P, m, k)), ALU.mult))
            for s in range(k):
                for i in range(m):
                    last = V.scalar_tensor_tensor(out=xp[:, t0 + i, :], in0=rows[:, i, s, 0:D], scalar=ef[:, i * k + s:i * k + s + 1],
                                                  in1=xp[:, t0 + i, :], op0=ALU.mult, op1=ALU.add)
                if s < k - 1:
                    link(last)
            link(last)

        def no_neighbours(L, tiles):
            if L == 1:
                eng.wait_ge(f["dense_used"], T)
                for t in tiles:
                    last = V.reciprocal(r.zr[:, t - ZERO_T:t - ZERO_T + 1], dense_out(t)[:, 0:1])
                link(last)
                zr = r.zr[:, tiles[0] - ZERO_T:tiles[-1] - ZERO_T + 1]
                link(V.tensor_tensor(zr, zr, r.empty[:, tiles[0]:tiles[-1] + 1], ALU.mult))
            else:
                eng.wait_ge(f["mean_ready"], 1 + (L + 1) // 2)
            for t in tiles:
                row, w = (dense_out(t)[:, 1:D + 1], r.zr[:, t - ZERO_T:t - ZERO_T + 1]) if L == 1 else (r.meanrow[:], r.empty[:, t:t + 1])
                last = V.scalar_tensor_tensor(out=xp[:, t, :], in0=row, scalar=w, in1=xp[:, t, :], op0=ALU.mult, op1=ALU.add)
            link(last)

        def dense(tiles):
            for j in tiles:
                eng.wait_ge(f["dense_added"], j + 1)
                b = db[j % DB]
                link(V.scalar_tensor_tensor(out=b, in0=b, scalar=SLOPE, in1=b, op0=ALU.mult, op1=ALU.max))
                V.scalar_tensor_tensor(out=b, in0=b, scalar=PENALTY[1], in1=m_row, op0=ALU.add, op1=ALU.subtract).then_inc(f["dense_shifted"], 1)

        scored = [0]
        for L in range(LAYERS):
            if L == 1:
                eng.wait_ge(f["projected_copied"], NG)
                link(V.reduce_max(r.dmax[:], vals[1][:, :, D + 1], AX.X))
                V.memset(r.scrap[:], 0.0).then_inc(f["target_max"], 1)
                eng.wait_ge(f["target_max_turned"], 1)
                link(V.reduce_max(r.dmax_one[:], r.ps[7][0:1, 0:P], AX.X))
                V.memset(r.scrap[:], 0.0).then_inc(f["target_max"], 1)
                eng.wait_ge(f["target_max_turned"], 2)
                link(V.tensor_copy(r.dmax_all[:], r.ps[7][:, P:P + 1]))
            for c in range(NC):
                if L == 1 and c == 0:
                    link(V.tensor_scalar(m_row, s_row, r.dmax_all[:, 0:1], None, ALU.add))
                    link(V.scalar_tensor_tensor(out=m_row, in0=m_row, scalar=SLOPE, in1=m_row, op0=ALU.mult, op1=ALU.max))
                    link(V.tensor_scalar(m_row, m_row, PENALTY[1], None, ALU.add))
                chunk_scores(L, c)
                if c and L < LAYERS - 1:
                    finish_norm(L + 1, c - 1)
                if L == 1:
                    dense(DENSE[c][:DENSE_FIRST])
                chunk_sum(L, c)
                V.memset(r.scrap[:], 0.0).then_inc(f["chunk_done"], 1)
                if L < LAYERS - 1:
                    stats(ORDER[L][c])
                if L == 1:
                    dense(DENSE[c][DENSE_FIRST:])
            if L < LAYERS - 1:
                finish_norm(L + 1, NC - 1)

    def scalar(eng):
        S = nc.scalar
        eng.wait_ge(f["x_stats_ready"], 1)
        S.activation(r.std[:], r.mv[:, :, 1], ACT.Sqrt, bias=r.eps[:, 0:1]).then_inc(f["x_std_ready"], 1)
        eng.wait_ge(f["x_norm_ready"], 1)
        with eng.Fori(0, T // 6) as i:
            for u in range(6):
                def sign(s):
                    S.activation(mask[u % 2][:, s, 0:SW], adjb[u % 3][:, s * SW:(s + 1) * SW], ACT.Sign, bias=r.minus_half[:, 0:1],
                                 accum_out=r.cnt[:, bass.ds(i * 6 + u, 1), s]).then_inc(f["mask_made"], 1)

                eng.wait_ge(f["adj_loaded%d" % (u % 3)], i * 32 + (16 * (u // 3) + 16))
                eng.wait_ge(f["mask_free"], i * 6 + (u + 1))
                sign(0)
                S.activation(r.query[:].rearrange("p (o d) -> p o d", o=1), rec[:, bass.ds(i * 6 + u, 1), 0:D], ACT.Relu, bias=r.shift[:, bass.ds(i * 6 + u, 1)],
                             scale=r.rstd[:, bass.ds(i * 6 + u, 1)]).then_inc(f["x_h_ready"], 1)
                sign(1)
                eng.wait_ge(f["x_turned"], i * 6 + (u + 1))
                S.copy(r.wa[:], r.ps[0][:, 0:D]).then_inc(f["x_turned_copied"], 1)
                eng.wait_ge(f["x_projected"], i * 6 + (u + 1))
                sign(2)
                S.copy(rec[:, bass.ds(i * 6 + u, 1), REC_Q:REC_Q + D], r.ps[2][:, 0:D].rearrange("p (o d) -> p o d", o=1)).then_inc(f["x_query_ready"], 1)

        def std(s, n):
            t0, m, k = CHUNKS[stage_order(s)[n]]
            eng.wait_ge(f["stats_ready"], (s - 1) * NC + n + 1)
            S.activation(r.std[:, t0:t0 + m], r.mv[:, t0:t0 + m, 1], ACT.Sqrt, bias=r.eps[:, 0:1]).then_inc(f["std_ready"], 1)

        def project(s, n):
            groups = chunk_groups(stage_order(s)[n])
            eng.wait_ge(f["norm_ready"], (s - 1) * NC + n + 1)
            for i in range(len(groups) + 2):
                if i < len(groups):
                    G = (s - 1) * NG + groups_before(s, n) + i
                    if G >= 2:
                        eng.wait_ge(f["turned"], G - 1)
                    for q, t in enumerate(groups[i]):
                        h = vals[1][:, t, 0:D] if s == 1 else hb[G % 2][:, q, :]
                        last = S.activation(h, xp[:, t, :], ACT.Relu, bias=r.shift[:, t:t + 1], scale=r.rstd[:, t:t + 1])
                    last.then_inc(f["h_ready"], 1)
                if 0 <= i - 1 < len(groups):
                    G = (s - 1) * NG + groups_before(s, n) + i - 1
                    w = len(groups[i - 1]) * D
                    eng.wait_ge(f["turned"], G + 1)
                    if G >= 2:
                        eng.wait_ge(f["projected"], G - 1)
                    S.copy(htb[G % 2][:, 0:w], r.ps[G % 2][:, 0:w]).then_inc(f["turned_copied"], 1)
                if 0 <= i - 2 < len(groups):
                    G = (s - 1) * NG + groups_before(s, n) + i - 2
                    ts = groups[i - 2]
                    eng.wait_ge(f["projected"], G + 1)
                    lo = D if s == 1 else 0
                    src = r.ps[2 + G % 2][:, 0:len(ts) * ROW].rearrange("p (t w) -> p t w", w=ROW)[:, :, lo:ROW]
                    dst = vals[s][:, ts[0]:ts[0] + len(ts), lo:ROW]
                    if s == 1 and ts[0] >= ZERO_T:
                        q = (ts[0] - ZERO_T) * P
                        S.copy(s_row[:, q:q + len(ts) * P], r.ps[5][:, 0:len(ts) * P])
                    S.copy(dst, src).then_inc(f["projected_copied"], 1)

        def mean(n, L):
            eng.wait_ge(f["mean_summed"], n)
            if n > 1:
                eng.wait_ge(f["chunk_done"], L * NC)
            S.mul(r.meanrow[:], r.ps[4][:, 0:D], 1.0 / N).then_inc(f["mean_ready"], 1)

        def dense_add(j):
            if j >= T:
                return
            if j >= DB:
                eng.wait_ge(f["dense_used"], j - DB + 1)
            S.activation(db[j % DB], s_row, ACT.Identity, bias=vals[1][:, j, D + 1:D + 2]).then_inc(f["dense_added"], 1)

        def dense_exp(j):
            eng.wait_ge(f["dense_shifted"], j + 1)
            S.activation(db[j % DB], db[j % DB], ACT.Exp).then_inc(f["dense_exp"], 1)

        scored = 0
        for L in range(LAYERS):
            if L != 1:
                mean(1 + (L + 1) // 2, L)
            for c in range(NC):
                g = L * NC + c
                m = GATHERS[ORDER[L][c]]
                if m:
                    scored += 1
                    eng.wait_ge(f["scores_ready"], scored)
                    S.activation(r.e[g % 2][:, 0:m], r.e[g % 2][:, 0:m], ACT.Exp, scale=SCALE[L]).then_inc(f["exp_ready"], 1)

                def dense(i):
                    for j in DENSE[c][i:i + 1]:
                        dense_add(j + 2)
                        dense_exp(j)

                if L == 1:
                    if c == 0:
                        dense_add(0)
                        dense_add(1)
                    for i in range(DENSE_FIRST):
                        dense(i)
                if L < LAYERS - 1:
                    if c:
                        project(L + 1, c - 1)
                    std(L + 1, c)
                if L == 1:
                    for i in range(DENSE_FIRST, len(DENSE[c])):
                        dense(i)
            if L < LAYERS - 1:
                project(L + 1, NC - 1)

    def tensor(eng):
        M = nc.tensor
        eng.wait_ge(r.weights_ready, r.WEIGHTS_READY)
        with eng.Fori(0, T) as t:
            eng.wait_ge(f["x_h_ready"], t + 1)
            M.transpose(r.ps[0][:, 0:P], r.query[:], r.ident[:]).then_inc(f["x_turned"], 1)
            eng.wait_ge(f["x_turned_copied"], t + 1)
            M.matmul(r.ps[2][:, 0:D], r.wa[:], r.w0[:], start=True, stop=True).then_inc(f["x_projected"], 1)
        eng.wait_ge(f["tri_ready"], 1)
        eng.wait_ge(f["classes_ready"], 1)
        CT = CLASSES * T
        ind = r.ind[:, :, :].rearrange("p c t -> p (c t)")
        M.matmul(r.ps[1][:, 0:CT], r.ones[:], ind, start=True, stop=True)
        M.matmul(r.ps[0][:, 0:CT], r.tri[:], ind, start=True, stop=True)
        M.matmul(r.ps[0][:, CT:CT + 1], r.ones[:], r.bad[:], start=True, stop=True).then_inc(f["ranks_ready"], 1)

        def project(s, n):
            groups = chunk_groups(stage_order(s)[n])
            for i in range(len(groups) + 1):
                if i < len(groups):
                    G = (s - 1) * NG + groups_before(s, n) + i
                    eng.wait_ge(f["h_ready"], G + 1)
                    if G >= 2:
                        eng.wait_ge(f["turned_copied"], G - 1)
                    for q, t in enumerate(groups[i]):
                        h = vals[1][:, t, 0:D] if s == 1 else hb[G % 2][:, q, :]
                        last = M.transpose(r.ps[G % 2][:, q * P:(q + 1) * P], h, r.ident[:])
                    last.then_inc(f["turned"], 1)
                if i >= 1:
                    G = (s - 1) * NG + groups_before(s, n) + i - 1
                    ts = groups[i - 1]
                    eng.wait_ge(f["turned_copied"], G + 1)
                    if G >= 2:
                        eng.wait_ge(f["projected_copied"], G - 1)
                    if s == 1 and ts[0] >= ZERO_T:
                        if ts[0] > ZERO_T:
                            eng.wait_ge(f["projected_copied"], G)
                        M.matmul(r.ps[5][:, 0:len(ts) * P], r.source_rep[:], htb[G % 2][:, 0:len(ts) * P], start=True, stop=True)
                    lo = D if s == 1 else 0
                    for q, t in enumerate(ts):
                        last = M.matmul(r.ps[2 + G % 2][:, q * ROW + lo:(q + 1) * ROW], htb[G % 2][:, q * P:(q + 1) * P],
                                        r.wext[s][:, lo:ROW], start=True, stop=True)
                    last.then_inc(f["projected"], 1)

        for L in range(LAYERS):
            if L != 1:
                if L == 0:
                    eng.wait_ge(f["inp_loaded"], 16)
                else:
                    eng.wait_ge(f["projected_copied"], L * NG)
                v = inp if L == 0 else vals[L]
                if L == 2:
                    eng.wait_ge(f["chunk_done"], 2 * NC)
                for t in range(T):
                    last = M.matmul(r.ps[4][:, 0:D], r.ones[:], v[:, t, 0:D], start=(t == 0), stop=(t == T - 1))
                last.then_inc(f["mean_summed"], 1)
            if L == 1:
                eng.wait_ge(f["target_max"], 1)
                M.transpose(r.ps[7][0:1, 0:P], r.dmax[:], r.ident[:]).then_inc(f["target_max_turned"], 1)
                eng.wait_ge(f["target_max"], 2)
                M.matmul(r.ps[7][:, P:P + 1], r.ones[0:1, :], r.dmax_one[:], start=True, stop=True).then_inc(f["target_max_turned"], 1)
            for c in range(NC):

                def dense(i):
                    for j in DENSE[c][i:i + 1]:
                        eng.wait_ge(f["dense_exp"], j + 1)
                        if j == 0:
                            eng.wait_ge(f["mean_ready"], 1)
                            for b in range(4, 7):
                                M.matmul(r.ps[b][:, :], r.zeros[:], db[0][:, 0:BANK], start=True, stop=False, skip_group_check=True)
                        for t in range(ZERO_T, T):
                            q = (t - ZERO_T) * P
                            last = M.matmul(dense_out(t), db[j % DB][:, q:q + P], v_odd1[:, j, 0:D + 1], start=False, stop=(j == T - 1), skip_group_check=True)
                        last.then_inc(f["dense_used"], 1)

                if L == 1:
                    for i in range(DENSE_FIRST):
                        dense(i)
                if L < LAYERS - 1 and c:
                    project(L + 1, c - 1)
                if L == 1:
                    for i in range(DENSE_FIRST, len(DENSE[c])):
                        dense(i)
            if L < LAYERS - 1:
                project(L + 1, NC - 1)

    return sp, gpsimd, vector, scalar, tensor
class Names:
    pass


def semaphores(nc, ctx, prefix, names):
    return {name: ctx.enter_context(nc.semaphore(prefix + name)) for name in names.split()}


def setup(nc, r, w0_d, attn_d, w2_d, a2_d, w3_d, a3_d):

    def sp(eng):
        eng.dma_start(r.w0[:], w0_d).then_inc(r.weights_loaded, 16)
        for k in range(2):
            eng.dma_start(r.wext[1][:, D + k:D + k + 1], attn_d[k * D:(k + 1) * D, :]).then_inc(r.weights_loaded, 16)
        for L, w, a in ((2, w2_d, a2_d), (3, w3_d, a3_d)):
            eng.dma_start(r.wext[L][:, 0:D], w).then_inc(r.weights_loaded, 16)
            eng.dma_start(r.arow[L][:], a.rearrange("n o -> (o n)").partition_broadcast(P)).then_inc(r.weights_loaded, 16)

    def gpsimd(eng):
        eng.memset(r.ident[:], 0.0).then_inc(r.ident_ready, 1)
        eng.wait_ge(r.ident_ready, 1)
        eng.affine_select(out=r.ident[:], in_=r.ident[:], compare_op=ALU.not_equal, fill=1.0, base=0,
                          pattern=[[-1, P]], channel_multiplier=1).then_inc(r.weights_ready, 1)

    def vector(eng):
        nc.vector.memset(r.eps[:], EPS).then_inc(r.eps_ready, 1)
        eng.wait_ge(r.weights_loaded, 16 * 7)
        n = 0
        for L in (2, 3):
            for k in range(2):
                nc.vector.tensor_tensor(r.wa[:], r.wext[L][:, 0:D], r.arow[L][:, k * D:(k + 1) * D], ALU.mult).then_inc(r.setup_step, 1)
                n += 1
                eng.wait_ge(r.setup_step, n)
                nc.vector.reduce_sum(r.wext[L][:, D + k:D + k + 1], r.wa[:], AX.X).then_inc(r.setup_step, 1)
                n += 1
                eng.wait_ge(r.setup_step, n)
        for L in (1, 2, 3):
            last = nc.vector.tensor_copy(r.target_rep[L][:], r.wext[L][:, D + 1:D + 2].to_broadcast((P, P)))
            last.then_inc(r.weights_ready, 1)
        nc.vector.tensor_copy(r.source_rep[:], r.wext[1][:, D:D + 1].to_broadcast((P, P))).then_inc(r.weights_ready, 1)
        for i in range(CLASSES - 1):
            nc.vector.memset(r.caps[:, i:i + 1], float(SLOT_TILES[CLASSES - 2 - i] * P))
        nc.vector.memset(r.onesrow[:], 1.0)

    return sp, gpsimd, vector


def gnn_kernel(nc, x, adj, inp, w0, attn, w2, a2, w3, a3, out):
    ctx = ExitStack()
    with ctx:
        def sb(name, shape, dt=F32):
            return ctx.enter_context(nc.sbuf_tensor(name, shape, dt))

        def dram(name, shape):
            return nc.dram_tensor(name, shape, F32, kind="Internal").ap()

        r = Names()
        r.weights_loaded, r.weights_ready, r.ident_ready, r.eps_ready, r.setup_step = (
            ctx.enter_context(nc.semaphore(n)) for n in ("weights_loaded", "weights_ready", "ident_ready", "eps_ready", "setup_step"))
        r.arena = sb("arena", [P, ARENA])
        r.region = [r.arena[:, i * N:(i + 1) * N] for i in range(7)]
        r.ps = [ctx.enter_context(nc.psum_tensor(f"ps{i}", [P, BANK], F32)) for i in range(8)]
        r.w0 = sb("w0", [P, D])
        r.wext = [None] + [sb(f"wext{L}", [P, D + 2]) for L in (1, 2, 3)]
        r.arow = [None, None] + [sb(f"arow{L}", [P, 2 * D]) for L in (2, 3)]
        r.target_rep = [None] + [sb(f"target_rep{L}", [P, P]) for L in (1, 2, 3)]
        r.wa, r.ident, r.query, r.agg = (sb(n, [P, P]) for n in ("wa", "ident", "query", "agg"))
        r.eps, r.scrap, r.rowmax, r.negmax, r.z, r.rz = (sb(n, [P, 1]) for n in ("eps", "scrap", "rowmax", "negmax", "z", "rz"))
        r.mean, r.var, r.std, r.rstd = (sb(n, [P, T]) for n in ("mean", "var", "std", "rstd"))
        r.score = sb("score", [P, T, 2])
        r.WEIGHTS_READY = 5
        r.tri, r.ones, r.zeros, r.source_rep = (sb(n, [P, P]) for n in ("tri", "ones", "zeros", "source_rep"))
        r.zr, r.dmax_one = sb("zr", [P, ZT]), sb("dmax_one", [1, 1])
        r.minus_half, r.dmax, r.dmax_all, r.bad = (sb(n, [P, 1]) for n in ("minus_half", "dmax", "dmax_all", "bad"))
        r.bad2 = sb("bad2", [P, 2])
        r.ones_needle = sb("ones_needle", [P, FOUND], BF16)
        r.seg_base, r.number, r.number2 = (sb(n, [P, SEG * FOUND]) for n in ("seg_base", "number", "number2"))
        r.found = sb("found", [P, SEG * FOUND], U32)
        r.best = sb("best", [P, 2 * FOUND])
        r.cnt = sb("cnt", [P, T, SEG])
        r.deg, r.posf, r.lowf, r.highf, r.has, r.empty, r.shift = (sb(n, [P, T]) for n in ("deg", "posf", "lowf", "highf", "has", "empty", "shift"))
        r.own_id, r.posi, r.low, r.high, r.place, r.own_p = (sb(n, [P, T], I32) for n in ("own_id", "posi", "low", "high", "place", "own_p"))
        r.ind = sb("ind", [P, CLASSES, T])
        r.tot, r.cum, r.onesrow = (sb(n, [P, CLASSES * T]) for n in ("tot", "cum", "onesrow"))
        r.caps, r.over = (sb(n, [P, CLASSES]) for n in ("caps", "over"))
        r.flag = sb("flag", [P, 1], I32)
        r.index0, r.index = (sb(n, [P, T, SLOTS], I32) for n in ("index0", "index"))
        r.pen = sb("pen", [P, T, SLOTS])
        r.bn = sb("bn", [P, T, 6])
        r.mv = sb("mv", [P, T, 2])
        r.e = [sb(f"e{i}", [P, CAP]) for i in range(2)]
        r.mx = sb("mx", [P, 16])
        r.meanrow = r.agg
        names = ("adj_loaded0 adj_loaded1 adj_loaded2 chunk_done classes_ready dense_added dense_exp "
                 "dense_shifted dense_used exp_ready flag_ready gathered0 gathered1 gathered2 "
                 "h_ready id_ready index_ready inp_loaded mask_free mask_made mean_ready "
                 "mean_summed norm_ready place_ready places_ready pool_step projected projected_copied "
                 "ranks_ready rec_loaded0 rec_loaded1 rec_loaded2 rec_scattered scores_ready search_step "
                 "stats_ready std_ready stored table0_written table_written target_max target_max_turned "
                 "tri_ready turned turned_copied vector_step x_h_ready x_loaded x_norm_ready "
                 "x_projected x_query_ready x_stats_ready x_std_ready x_turned x_turned_copied ")
        r.fast = semaphores(nc, ctx, "f_", names)
        rec_d = dram("records", (N, REC))
        tab_d = [dram(f"table{L}", (N, ROW if L else ROW0)) for L in range(LAYERS)]
        r.general = semaphores(nc, ctx, "g_", "x_loaded adj_loaded penalty_ready row_done stored vector_step var_ready std_ready h_ready "
                               "psum_filled psum_emptied query_ready score_filled scores_ready masked probs_ready probs_turned turned_copied aggregated")
        setup_sp, setup_pool, setup_dve = setup(nc, r, w0, attn, w2, a2, w3, a3)
        g_sp, g_dve, g_act, g_pe = general_path(nc, r, adj, x, inp, out)
        f_sp, f_pool, f_dve, f_act, f_pe = fast_path(nc, r, adj, x, inp, out, rec_d, tab_d)
        block = ctx.enter_context(nc.Block())

        def otherwise(eng, program):
            eng.wait_ge(r.fast["stored"], 16 * T)
            no_room = eng.value_load(r.flag[0:1, 0:1])
            with eng.If(no_room > 0):
                program(eng)

        @block.sync
        def _(sp):
            setup_sp(sp)
            f_sp(sp)
            otherwise(sp, g_sp)

        @block.gpsimd
        def _(pool):
            setup_pool(pool)
            f_pool(pool)

        @block.vector
        def _(dve):
            setup_dve(dve)
            f_dve(dve)
            otherwise(dve, g_dve)

        @block.scalar
        def _(act):
            act.wait_ge(r.eps_ready, 1)
            f_act(act)
            otherwise(act, g_act)

        @block.tensor
        def _(pe):
            f_pe(pe)
            otherwise(pe, g_pe)


_INS = ["x", "adj", "L0_gnn_input", "L0_gnn_weight", "L1_gnn_attn", "L2_gnn_W", "L2_gnn_a", "L3_gnn_Ws", "L3_gnn_a"]


def kernel(**inputs):
    import numpy as _np
    import concourse.bacc as _bacc
    from concourse import mybir as _mybir
    from concourse.bass_utils import run_bass_kernel_spmd as _run

    nc = _bacc.Bacc("TRN2", target_bir_lowering=False, num_devices=1)
    arrays, args = {}, []
    for name in _INS:
        a = _np.ascontiguousarray(inputs[name])
        arrays[f"in_{name}"] = a
        args.append(nc.dram_tensor(f"in_{name}", a.shape, _mybir.dt.from_np(a.dtype), kind="ExternalInput").ap())
    args.append(nc.dram_tensor("out_x", (N, D), _mybir.dt.float32, kind="ExternalOutput").ap())
    gnn_kernel(nc, *args)
    r = _run(nc, [arrays], core_ids=[0])
    return r.results[0]["out_x"]
```

```python
import concourse.bass as bass
from concourse import mybir
from contextlib import ExitStack

F32, I32, U32, BF16 = mybir.dt.float32, mybir.dt.int32, mybir.dt.uint32, mybir.dt.bfloat16
ALU, ACT, AX = mybir.AluOpType, mybir.ActivationFunctionType, mybir.AxisListType

P = 128
N = 6144
D = 128
T = N // P
BANK = 512
CH = N // BANK
TPC = BANK // P
LAYERS = 4
SLOPE = 0.2
EPS = 1e-5
PENALTY = [-1e30, -1e9, -9e15, -9e15]
SCALE = [1.0 / 0.07, 1.0, 1.0, 1.0]


def general_path(nc, r, adj_d, x_d, inp_d, out_d):
    X, H, HT, VAL, COL, ADJ, PEN = r.region
    E, QT, PT = HT, H, PEN
    x3 = lambda b: b[:, :].rearrange("p (t d) -> p t d", d=D)
    adj_v = adj_d.rearrange("(p t) j -> p t j", t=T)
    row_major = lambda d: d.rearrange("(p t) d -> p t d", t=T)
    g = r.general

    def values(L):
        return x3(H) if L == 1 else x3(VAL)

    def sp(eng):
        eng.dma_start(x3(X), row_major(x_d)).then_inc(g["x_loaded"], 16)
        eng.dma_start(x3(VAL), row_major(inp_d)).then_inc(g["x_loaded"], 16)
        for L in range(LAYERS):
            with eng.Fori(0, T) as t:
                eng.wait_ge(g["penalty_ready"], t + (L * T + 1))
                eng.dma_start(ADJ[:, :].rearrange("p (o j) -> p o j", o=1).bitcast(I32),
                              adj_v[:, bass.ds(t, 1), :]).then_inc(g["adj_loaded"], 16)
        eng.wait_ge(g["row_done"], LAYERS * T)
        eng.dma_start(row_major(out_d), x3(X)).then_inc(g["stored"], 16)
        eng.wait_ge(g["stored"], 16)

    def vector(eng):
        n = [0]

        def link(ins):
            n[0] += 1
            ins.then_inc(g["vector_step"], 1)
            eng.wait_ge(g["vector_step"], n[0])

        nc.vector.memset(r.scrap[:], 0.0).then_inc(g["penalty_ready"], 1)
        eng.wait_ge(g["x_loaded"], 32)
        evac = 0
        for L in range(LAYERS):
            h = x3(H)
            if L:
                eng.wait_ge(g["row_done"], L * T)
            link(nc.vector.reduce_sum(r.mean[:], x3(X), AX.X))
            link(nc.vector.tensor_scalar(r.mean[:], r.mean[:], 1.0 / D, None, ALU.mult))
            link(nc.vector.tensor_tensor(h, x3(X), r.mean[:].unsqueeze(2).to_broadcast((P, T, D)), ALU.subtract))
            link(nc.vector.tensor_tensor(x3(PEN), h, h, ALU.mult))
            nc.vector.reduce_sum(r.var[:], x3(PEN), AX.X).then_inc(g["var_ready"], 1)
            eng.wait_ge(g["std_ready"], L + 1)
            link(nc.vector.reciprocal(r.rstd[:], r.std[:]))
            nc.vector.scalar_tensor_tensor(out=h, in0=h, scalar=0.0, in1=r.rstd[:].unsqueeze(2).to_broadcast((P, T, D)),
                                           op0=ALU.max, op1=ALU.mult).then_inc(g["h_ready"], 1)
            for c in range(CH):
                eng.wait_ge(g["psum_filled"], evac + 1)
                nc.vector.tensor_copy(HT[:, c * BANK:(c + 1) * BANK], r.ps[c % 4][:, :]).then_inc(g["psum_emptied"], 1)
                evac += 1
            if L == 0:
                for dst in (QT, COL):
                    for c in range(CH):
                        eng.wait_ge(g["psum_filled"], evac + 1)
                        nc.vector.tensor_copy(dst[:, c * BANK:(c + 1) * BANK], r.ps[c % 4][:, :]).then_inc(g["psum_emptied"], 1)
                        evac += 1
            else:
                for t in range(T):
                    eng.wait_ge(g["psum_filled"], evac + 1)
                    if L > 1:
                        nc.vector.tensor_copy(x3(VAL)[:, t, :], r.ps[t % 4][:, 0:D])
                    nc.vector.tensor_copy(r.score[:, t, :], r.ps[t % 4][:, D:D + 2]).then_inc(g["psum_emptied"], 1)
                    evac += 1
                for c in range(CH):
                    eng.wait_ge(g["psum_filled"], evac + 1)
                    nc.vector.tensor_copy(COL[:, c * BANK:(c + 1) * BANK], r.ps[c % 4][:, :]).then_inc(g["psum_emptied"], 1)
                    evac += 1
            link(nc.vector.memset(r.scrap[:], 0.0))
            if L:
                eng.wait_ge(g["psum_emptied"], evac)
            per = 6 if L else 4
            base = n[0]
            with eng.Fori(0, T) as t:
                k = [0]

                def step(ins):
                    k[0] += 1
                    ins.then_inc(g["vector_step"], 1)
                    eng.wait_ge(g["vector_step"], t * per + (base + k[0]))

                eng.wait_ge(g["adj_loaded"], t * 16 + 16 * (L * T + 1))
                nc.vector.tensor_scalar(PEN[:, :], ADJ[:, :].bitcast(I32), 0.0, PENALTY[L], ALU.is_le, ALU.mult).then_inc(g["penalty_ready"], 1)
                if L == 0:
                    nc.vector.tensor_copy(r.query[:], QT[:, bass.ds(t * P, P)]).then_inc(g["query_ready"], 1)
                eng.wait_ge(g["penalty_ready"], t + (L * T + 2))
                if L:
                    step(nc.vector.tensor_scalar(E[:, :], COL[:, :], r.score[:, bass.ds(t, 1), 0], None, ALU.add))
                    step(nc.vector.scalar_tensor_tensor(out=E[:, :], in0=E[:, :], scalar=SLOPE, in1=E[:, :], op0=ALU.mult, op1=ALU.max))
                else:
                    eng.wait_ge(g["scores_ready"], t * CH + CH)
                step(nc.vector.tensor_tensor(E[:, :].rearrange("i (t p) -> i t p", t=T), E[:, :].rearrange("i (t p) -> i t p", t=T),
                                             PEN[:, :].rearrange("i (p t) -> i t p", t=T), ALU.add))
                step(nc.vector.reduce_max(r.rowmax[:], E[:, :], AX.X))
                nc.vector.tensor_scalar(E[:, :], E[:, :], r.rowmax[:, 0:1], SCALE[L], ALU.subtract, ALU.mult).then_inc(g["masked"], 1)
                eng.wait_ge(g["aggregated"], t + (L * T + 1))
                step(nc.vector.reciprocal(r.rz[:], r.z[:]))
                step(nc.vector.tensor_scalar(r.agg[:], r.ps[4][:, 0:D], r.rz[:, 0:1], None, ALU.mult))
                xt = x3(X)[:, bass.ds(t, 1), :]
                nc.vector.tensor_tensor(xt, xt, r.agg[:].rearrange("p (o d) -> p o d", o=1), ALU.add).then_inc(g["row_done"], 1)
                assert k[0] == per
            n[0] = base + T * per

    def scalar(eng):
        eng.wait_ge(r.eps_ready, 1)
        for L in range(LAYERS):
            eng.wait_ge(g["var_ready"], L + 1)
            nc.scalar.activation(r.std[:], r.var[:], ACT.Sqrt, bias=r.eps[:, 0:1], scale=1.0 / D).then_inc(g["std_ready"], 1)
            with eng.Fori(0, T) as t:
                if L == 0:
                    for c in range(CH):
                        eng.wait_ge(g["score_filled"], t * CH + (c + 1))
                        nc.scalar.copy(E[:, c * BANK:(c + 1) * BANK], r.ps[c % 4][:, :]).then_inc(g["scores_ready"], 1)
                eng.wait_ge(g["masked"], t + (L * T + 1))
                nc.scalar.activation(E[:, :], E[:, :], ACT.Exp, accum_out=r.z[:, 0:1]).then_inc(g["probs_ready"], 1)
                for c in range(CH):
                    eng.wait_ge(g["probs_turned"], t * CH + (L * T * CH + c + 1))
                    nc.scalar.copy(PT[:, c * BANK:(c + 1) * BANK], r.ps[c % 4][:, :]).then_inc(g["turned_copied"], 1)

    def tensor(eng):
        eng.wait_ge(r.weights_ready, r.WEIGHTS_READY)
        filled = 0

        def fill(bank_free):
            if bank_free > 4:
                eng.wait_ge(g["psum_emptied"], bank_free - 4)

        for L in range(LAYERS):
            eng.wait_ge(g["h_ready"], L + 1)
            if L:
                eng.wait_ge(g["turned_copied"], L * T * CH)
            for c in range(CH):
                fill(filled + 1)
                for q in range(TPC):
                    t = c * TPC + q
                    last = nc.tensor.transpose(r.ps[c % 4][:, q * P:(q + 1) * P], x3(H)[:, t, :], r.ident[:])
                last.then_inc(g["psum_filled"], 1)
                filled += 1
            eng.wait_ge(g["psum_emptied"], filled)
            if L == 0:
                for c in range(CH):
                    fill(filled + 1)
                    nc.tensor.matmul(r.ps[c % 4][:, :], r.w0[:], HT[:, c * BANK:(c + 1) * BANK], start=True, stop=True).then_inc(g["psum_filled"], 1)
                    filled += 1
                for c in range(CH):
                    fill(filled + 1)
                    for q in range(TPC):
                        last = nc.tensor.transpose(r.ps[c % 4][:, q * P:(q + 1) * P], x3(VAL)[:, c * TPC + q, :], r.ident[:])
                    last.then_inc(g["psum_filled"], 1)
                    filled += 1
            else:
                for t in range(T):
                    fill(filled + 1)
                    lo = D if L == 1 else 0
                    nc.tensor.matmul(r.ps[t % 4][:, lo:D + 2], HT[:, t * P:(t + 1) * P], r.wext[L][:, lo:D + 2], start=True, stop=True).then_inc(g["psum_filled"], 1)
                    filled += 1
                for c in range(CH):
                    fill(filled + 1)
                    nc.tensor.matmul(r.ps[c % 4][:, :], r.target_rep[L][:], HT[:, c * BANK:(c + 1) * BANK], start=True, stop=True).then_inc(g["psum_filled"], 1)
                    filled += 1
            eng.wait_ge(g["psum_emptied"], filled)
            with eng.Fori(0, T) as t:
                if L == 0:
                    eng.wait_ge(g["query_ready"], t + 1)
                    for c in range(CH):
                        if c >= 4:
                            eng.wait_ge(g["scores_ready"], t * CH + (c - 3))
                        nc.tensor.matmul(r.ps[c % 4][:, :], r.query[:], COL[:, c * BANK:(c + 1) * BANK], start=True, stop=True).then_inc(g["score_filled"], 1)
                eng.wait_ge(g["probs_ready"], t + (L * T + 1))
                for c in range(CH):
                    if c >= 4:
                        eng.wait_ge(g["turned_copied"], t * CH + (L * T * CH + c - 3))
                    for q in range(TPC):
                        b = c * TPC + q
                        last = nc.tensor.transpose(r.ps[c % 4][:, q * P:(q + 1) * P], E[:, b * P:(b + 1) * P], r.ident[:])
                    last.then_inc(g["probs_turned"], 1)
                eng.wait_ge(g["turned_copied"], t * CH + (L * T * CH + CH))
                for b in range(T):
                    last = nc.tensor.matmul(r.ps[4][:, 0:D], PT[:, b * P:(b + 1) * P], values(L)[:, b, :], start=(b == 0), stop=(b == T - 1))
                last.then_inc(g["aggregated"], 1)

    return sp, vector, scalar, tensor
ARENA = 7 * N + 840

SEG = 3
SW = N // SEG
FOUND = 8
SLOTS = 12
SLOT_TILES = [43, 30, 17, 8, 4, 2] + [1] * (SLOTS - 6)
ZERO_T = 40
ZT = T - ZERO_T
ZERO_ROWS = 960
SKIP = ZT * P - ZERO_ROWS
CLASSES = 8
REC = 272
REC_Q, REC_NB, REC_ID = D, 2 * D, 2 * D + SLOTS
ROW = D + 2
ROW0 = D + 1
CHUNKS = [(0, 1, 12), (1, 1, 6), (2, 2, 5), (4, 4, 4), (8, 5, 3), (13, 4, 3), (17, 7, 2), (24, 6, 2), (30, 5, 1), (35, 5, 1), (40, 4, 1), (44, 4, 0)]
NC = len(CHUNKS)
RING = 3
CAP = 20
GROUP = 3


def chunk_tiles(c):
    t0, n, k = CHUNKS[c]
    return [t for t in range(t0, t0 + n) if t < SLOT_TILES[0]]


def chunk_groups(c):
    t0, n, k = CHUNKS[c]
    return [list(range(t, min(t + GROUP, t0 + n))) for t in range(t0, t0 + n, GROUP)]


ORDER = [[8, 9, 7, 10, 11, 6, 5, 4, 3, 2, 1, 0], [8, 9, 7, 6, 5, 4, 3, 2, 1, 0, 10, 11]] + 2 * [[8, 9, 7, 10, 11, 6, 5, 4, 3, 2, 1, 0]]
PARTS = [(30, 35), (35, 40), (24, 30), (40, 48), (0, 24)]
NG = sum(len(chunk_groups(c)) for c in range(NC))
TURN = [[sum(CHUNKS[c][2] > 0 for c in ORDER[L][:n]) + L * (NC - 1) for n in range(NC)] for L in range(LAYERS)]
GATHERS = [len(chunk_tiles(c)) * CHUNKS[c][2] for c in range(NC)]


AHEAD = 2
DENSE_FIRST = 3


def stage_order(s):
    return ORDER[s - 1]


def groups_before(s, n):
    return sum(len(chunk_groups(c)) for c in stage_order(s)[:n])


DENSE = [list(range(n * T // (NC - 2), (n + 1) * T // (NC - 2))) for n in range(NC - 2)] + 2 * [[]]


def fast_path(nc, r, adj_d, x_d, inp_d, out_d, rec_d, tab_d):
    f = r.fast
    A = r.arena
    at = [0]

    def take(start, size):
        assert start + size <= ARENA, (start, size)
        return A[:, start:start + size]

    adjb = [take(i * N, N).bitcast(I32) for i in range(3)]
    mask_w = SEG * (SW + FOUND) // 2
    mask = [take(3 * N + i * mask_w, mask_w).bitcast(BF16).rearrange("p (s w) -> p s w", s=SEG) for i in range(2)]
    o = 3 * N + 2 * mask_w
    rec = take(o, T * REC).rearrange("p (t c) -> p t c", t=T)
    o_inp = o + T * REC
    inp = take(o_inp, T * ROW0).rearrange("p (t c) -> p t c", t=T)
    recp = take(0, T * REC).rearrange("p (t c) -> p t c", t=T)
    xp = recp[:, :, 0:D]
    o = T * REC
    v_even1 = take(o, T * (ROW + 1)).rearrange("p (t c) -> p t c", t=T)
    o += T * (ROW + 1)
    v_odd1 = take(o, T * (ROW + 1)).rearrange("p (t c) -> p t c", t=T)
    o += T * (ROW + 1)
    v_even, v_odd = v_even1[:, :, 1:], v_odd1[:, :, 1:]
    gat = [take(o + i * CAP * ROW, CAP * ROW) for i in range(RING)]
    o += RING * CAP * ROW
    hb = [take(o + i * GROUP * D, GROUP * D).rearrange("p (t c) -> p t c", t=GROUP) for i in range(2)]
    o += 2 * GROUP * D
    htb = [take(o + i * GROUP * D, GROUP * D) for i in range(2)]
    o += 2 * GROUP * D
    prod = take(o, CAP * D)
    assert o + CAP * D <= o_inp
    ZW = ZT * P
    s_row, m_row, *db = [take(o_inp + i * ZW, ZW) for i in range(6)] + [r.dense_more[:]]
    DB = len(db)
    vals = [None, v_odd, v_even, v_odd]
    row_major = lambda d: d.rearrange("(p t) d -> p t d", t=T)
    adj_v = adj_d.rearrange("(p t) j -> p t j", t=T)

    def dense_out(t):
        q = t - ZERO_T
        return r.ps[4 + q // 3][:, q % 3 * (D + 1):(q % 3 + 1) * (D + 1)]

    def sp(eng):
        eng.dma_start(rec[:, :, 0:D], row_major(x_d)).then_inc(f["x_loaded"], 16)
        for t in range(3):
            for s in range(SEG):
                eng.dma_start(adjb[t][:, s * SW:(s + 1) * SW].rearrange("p (o j) -> p o j", o=1),
                              adj_v[:, t:t + 1, s * SW:(s + 1) * SW]).then_inc(f["adj_loaded%d%d" % (t, s)], 16)
        eng.dma_start(inp[:, :, 0:D], row_major(inp_d)).then_inc(f["inp_loaded"], 16)
        with eng.Fori(0, T // 3 - 1) as i:
            for b in range(3):
                for s in range(SEG):
                    eng.wait_ge(f["mask_made"], i * (3 * SEG) + (b * SEG + s + 1))
                    eng.dma_start(adjb[b][:, s * SW:(s + 1) * SW].rearrange("p (o j) -> p o j", o=1),
                                  adj_v[:, bass.ds(i * 3 + (b + 3), 1), s * SW:(s + 1) * SW]).then_inc(f["adj_loaded%d%d" % (b, s)], 16)
        eng.wait_ge(f["place_ready"], 1)
        eng.dma_start(row_major(tab_d[0]), inp).then_inc(f["table0_written"], 16)
        eng.wait_ge(f["rec_scattered"], 16 * T)
        for i, (lo, hi) in enumerate(PARTS):
            eng.dma_start(recp[:, lo:hi, :], row_major(rec_d)[:, lo:hi, :]).then_inc(f["rec_loaded%d" % i], 16)
        for s in (1, 2, 3):
            for i, c in enumerate(stage_order(s)):
                t0, n, k = CHUNKS[c]
                eng.wait_ge(f["projected_copied"], (s - 1) * NG + groups_before(s, i + 1))
                eng.dma_start(row_major(tab_d[s])[:, t0:t0 + n, :], vals[s][:, t0:t0 + n, :]).then_inc(f["table_written"], 16)

    def gpsimd(eng):
        nc.gpsimd.iota(r.own_id[:], pattern=[[1, T]], base=0, channel_multiplier=T).then_inc(f["id_ready"], 1)
        eng.memset(r.tri[:], 1.0).then_inc(f["pool_step"], 1)
        eng.wait_ge(f["pool_step"], 1)
        eng.affine_select(out=r.tri[:], in_=r.tri[:], compare_op=ALU.is_gt, fill=0.0, base=0,
                          pattern=[[1, P]], channel_multiplier=-1).then_inc(f["tri_ready"], 1)
        eng.wait_ge(f["place_ready"], 1)
        for t in range(T):
            nc.gpsimd.indirect_dma_start(out=rec_d[:, :], out_offset=bass.IndirectOffsetOnAxis(ap=r.place[:, t:t + 1], axis=0),
                                         in_=rec[:, t, :], in_offset=None).then_inc(f["rec_scattered"], 16)
        for L in range(LAYERS):
            if L == 0:
                eng.wait_ge(f["index_ready"], 1)
                eng.wait_ge(f["table0_written"], 16)
            else:
                eng.wait_ge(f["places_ready"], NC - 1)
                eng.wait_ge(f["table_written"], 16 * NC * L)
            width = ROW if L else ROW0
            index = r.index if L else r.index0
            for n, c in enumerate(ORDER[L]):
                k = CHUNKS[c][2]
                g = TURN[L][n]
                if L == 0 and n:
                    eng.wait_ge(f["index_ready"], 1 + [lo <= CHUNKS[c][0] < hi for lo, hi in PARTS].index(True))
                if k and g >= RING:
                    eng.wait_ge(f["rows_used"], g - RING + 1)
                for i, t in enumerate(chunk_tiles(c)):
                    for s in range(k):
                        w = (i * k + s) * width
                        nc.gpsimd.indirect_dma_start(out=gat[g % RING][:, w:w + width], out_offset=None, in_=tab_d[L][:, :],
                                                     in_offset=bass.IndirectOffsetOnAxis(ap=index[:, t, s:s + 1], axis=0)
                                                     ).then_inc(f["gathered%d" % (g % RING)], 16)
                if L == LAYERS - 1 and n >= 2:
                    store(eng, n - 2)
        for n in (NC - 2, NC - 1):
            store(eng, n)
        eng.wait_ge(f["stored"], 16 * T)

    def store(eng, n):
        eng.wait_ge(f["chunk_done"], (LAYERS - 1) * NC + n + 1)
        c = ORDER[LAYERS - 1][n]
        for t in range(CHUNKS[c][0], CHUNKS[c][0] + CHUNKS[c][1]):
            nc.gpsimd.indirect_dma_start(out=out_d[:, :], out_offset=bass.IndirectOffsetOnAxis(ap=r.own_p[:, t:t + 1], axis=0),
                                         in_=xp[:, t, :], in_offset=None).then_inc(f["stored"], 16)

    def vector(eng):
        n = [0]

        def link(ins):
            n[0] += 1
            ins.then_inc(f["vector_step"], 1)
            eng.wait_ge(f["vector_step"], n[0])

        V = nc.vector
        V.memset(r.minus_half[:], -0.5)
        V.memset(r.ones_needle[:], 1.0)
        V.memset(r.ones[:], 1.0)
        V.memset(r.ones_half[:], 1.0)
        V.memset(r.zeros[:], 0.0)
        for s in range(SEG):
            last = V.memset(r.seg_base[:, :, s * FOUND:(s + 1) * FOUND], float(s * SW + 1))
        link(last)
        for b in range(2):
            V.memset(mask[b][:, :, SW:], 1.0).then_inc(f["mask_free"], 1)
        eng.wait_ge(f["x_loaded"], 16)
        for t in range(T):
            last = V.bn_stats(r.bn[:, t, :], rec[:, t, 0:D])
        link(last)
        for t in range(T):
            last = V.bn_aggr(r.mv[:, t, :], r.bn[:, t, :])
        last.then_inc(f["x_stats_ready"], 1)
        eng.wait_ge(f["x_std_ready"], 1)
        link(V.reciprocal(r.rstd[:], r.std[:]))
        V.scalar_tensor_tensor(out=r.shift[:], in0=r.mv[:, :, 0], scalar=-1.0, in1=r.rstd[:], op0=ALU.mult, op1=ALU.mult).then_inc(f["x_norm_ready"], 1)
        eng.wait_ge(f["id_ready"], 1)
        V.tensor_copy(rec[:, :, REC_ID], r.own_id[:])
        V.memset(rec[:, :, REC_ID + 1:REC], 0.0)
        V.memset(r.cum[:, 0:1], 0.0)
        with eng.Fori(0, T // 2) as i:
            eng.sem_clear(f["search_step"])
            k = [0]

            def step(ins):
                k[0] += 1
                ins.then_inc(f["search_step"], 1)
                return k[0]

            for b in range(2):
                for s in range(SEG):
                    eng.wait_ge(f["mask_made"], i * (2 * SEG) + (b * SEG + s + 1))
                    V.memset(r.seg_mark[:, b * SEG + s:b * SEG + s + 1], 0.0)
                    last = V.max_index(r.found[:, b, s * FOUND:(s + 1) * FOUND], r.ones_needle[:], mask[b][:, s, :])
                last.then_inc(f["mask_free"], 1)
            eng.wait_ge(f["mask_free"], i * 2 + 4)
            V.memset(r.scrap[:], 0.0)
            done = step(V.tensor_tensor(r.number[:], r.found[:], r.seg_base[:], ALU.add))
            eng.wait_ge(f["search_step"], done)
            done = step(V.scalar_tensor_tensor(out=r.number[:], in0=r.found[:], scalar=float(SW), in1=r.number[:], op0=ALU.is_lt, op1=ALU.mult))
            eng.wait_ge(f["search_step"], done)
            high = [step(V.max(out=r.best[:, b, 0:8], in_=r.number[:, b, :])) for b in range(2)]
            rest = []
            for b in range(2):
                eng.wait_ge(f["search_step"], high[b])
                rest.append(step(V.match_replace(out=r.number2[:, b, :], in_to_replace=r.best[:, b, 0:8], in_values=r.number[:, b, :], imm_value=0.0)))
            for b in range(2):
                eng.wait_ge(f["search_step"], rest[b])
                done = step(V.max(out=r.best[:, b, 8:16], in_=r.number2[:, b, :]))
            eng.wait_ge(f["search_step"], done)
            done = step(V.tensor_copy(rec[:, bass.ds(i * 2, 2), REC_NB:REC_NB + SLOTS], r.best[:, :, 0:SLOTS]))
            eng.wait_ge(f["search_step"], done)
        eng.wait_ge(f["mask_made"], T * SEG)
        link(V.reduce_sum(r.deg[:], r.cnt[:], AX.X))
        link(V.tensor_scalar(r.deg[:], r.deg[:], float(N), 0.5, ALU.add, ALU.mult))
        for i in range(CLASSES):
            deg = CLASSES - 1 - i
            last = V.tensor_scalar(r.ind[:, i, :], r.deg[:], float(deg), None, ALU.is_ge if i == 0 else ALU.is_equal)
        link(last)
        V.memset(r.scrap[:], 0.0).then_inc(f["classes_ready"], 1)
        eng.wait_ge(f["ranks_ready"], 1)
        ind = r.ind[:, :, :].rearrange("p c t -> p (c t)")
        CT = CLASSES * T
        link(V.tensor_tensor_scan(out=r.cum[:, 1:CT + 1], data0=r.onesrow[:], data1=r.ps[1][:, 0:CT], initial=0.0, op0=ALU.mult, op1=ALU.add))
        link(V.tensor_tensor(r.rank[:], r.cum[:, 0:CT], r.ps[0][:, 0:CT], ALU.add))
        link(V.tensor_tensor(r.rank[:], r.rank[:], ind, ALU.mult))
        link(V.reduce_sum(r.posf[:], r.rank[:, :].rearrange("p (c t) -> p t c", t=T), AX.X))
        link(V.tensor_copy(r.posi[:], r.posf[:]))
        V.tensor_scalar(r.low[:], r.posi[:], P - 1, None, ALU.bitwise_and)
        link(V.tensor_scalar(r.high[:], r.posi[:], 7, None, ALU.arith_shift_right))
        eng.wait_ge(f["inp_loaded"], 16)
        eng.wait_ge(f["x_query_ready"], T)
        link(V.scalar_tensor_tensor(out=inp[:, :, D], in0=r.low[:], scalar=float(T), in1=r.high[:], op0=ALU.mult, op1=ALU.add))
        V.tensor_copy(r.place[:], inp[:, :, D]).then_inc(f["place_ready"], 1)
        link(V.tensor_scalar(r.cnt[:], r.cnt[:], float(2 * FOUND - SW), None, ALU.is_gt))
        link(V.tensor_reduce(r.bad2[:, 0:1], r.cnt[:], AX.XY, ALU.max))
        link(V.tensor_scalar(r.deg[:], r.deg[:], float(SLOTS), None, ALU.is_gt))
        link(V.reduce_max(r.bad2[:, 1:2], r.deg[:], AX.X))
        V.tensor_tensor(r.bad[:], r.bad2[:, 0:1], r.bad2[:, 1:2], ALU.add).then_inc(f["bad_ready"], 1)
        eng.wait_ge(f["bad_summed"], 1)
        cum_end = r.cum[:, 1:CT + 1].rearrange("p (c t) -> p c t", t=T)[:, :, T - 1]
        link(V.tensor_tensor(r.over[:, 0:CLASSES - 1], cum_end[:, 0:CLASSES - 1], r.caps[:, 0:CLASSES - 1], ALU.is_gt))
        link(V.tensor_scalar(r.over[:, CLASSES - 1:CLASSES], cum_end[:, CLASSES - 2:CLASSES - 1], float(N - ZERO_ROWS), None, ALU.is_lt))
        link(V.reduce_sum(r.bad2[:, 0:1], r.over[:], AX.X))
        link(V.tensor_tensor(r.bad2[:, 1:2], r.bad2[:, 0:1], r.ps[2][:, 0:1], ALU.add))
        V.tensor_copy(r.flag[:], r.bad2[:, 1:2]).then_inc(f["flag_ready"], 1)
        for i, (lo, hi) in enumerate(PARTS):
            eng.wait_ge(f["rec_loaded%d" % i], 16)
            nb = recp[:, lo:hi, REC_NB:REC_NB + SLOTS]
            V.tensor_scalar(r.index0[:, lo:hi, :], nb, -1.0, 0.0, ALU.add, ALU.max).then_inc(f["index_ready"], 1)
            V.tensor_copy(r.own_p[:, lo:hi], recp[:, lo:hi, REC_ID])
            V.tensor_scalar(r.pen[:, lo:hi, :], nb, 0.0, -1e30, ALU.is_le, ALU.mult)
            V.tensor_scalar(r.has[:, lo:hi], recp[:, lo:hi, REC_NB], 0.0, None, ALU.is_gt)
            link(V.tensor_scalar(r.empty[:, lo:hi], recp[:, lo:hi, REC_NB], 0.0, None, ALU.is_le))
        V.memset(v_odd1[:, :, 0:1], 1.0)

        def stats(c):
            t0, m, k = CHUNKS[c]
            for t in range(t0, t0 + m):
                last = V.bn_stats(r.bn[:, t, :], xp[:, t, :])
            link(last)
            for t in range(t0, t0 + m):
                last = V.bn_aggr(r.mv[:, t, :], r.bn[:, t, :])
            last.then_inc(f["stats_ready"], 1)

        def finish_norm(s, n_):
            t0, m, k = CHUNKS[stage_order(s)[n_]]
            eng.wait_ge(f["std_ready"], (s - 1) * NC + n_ + 1)
            link(V.reciprocal(r.rstd[:, t0:t0 + m], r.std[:, t0:t0 + m]))
            V.scalar_tensor_tensor(out=r.shift[:, t0:t0 + m], in0=r.mv[:, t0:t0 + m, 0], scalar=-1.0, in1=r.rstd[:, t0:t0 + m],
                                   op0=ALU.mult, op1=ALU.mult).then_inc(f["norm_ready"], 1)

        arrived = [0] * RING

        def chunk_scores(L, at_):
            c = ORDER[L][at_]
            t0, m, k = CHUNKS[c]
            m = len(chunk_tiles(c))
            g = TURN[L][at_]
            if not k:
                return
            arrived[g % RING] += 16 * GATHERS[c]
            w = ROW if L else ROW0
            rows = gat[g % RING][:, 0:m * k * w].rearrange("p (t k w) -> p t k w", t=m, k=k)
            e = r.e[g % 2][:, 0:m * k].rearrange("p (t k) -> p t k", k=k)
            eng.wait_ge(f["gathered%d" % (g % RING)], arrived[g % RING])
            if L == 0:
                q = recp[:, t0:t0 + m, REC_Q:REC_Q + D].unsqueeze(2).to_broadcast((P, m, k, D))
                pr = prod[:, 0:m * k * D].rearrange("p (t k d) -> p t k d", t=m, k=k)
                link(V.tensor_tensor(pr, rows[:, :, :, 0:D], q, ALU.mult))
                V.tensor_copy(r.index[:, t0:t0 + m, 0:k], rows[:, :, :, D]).then_inc(f["places_ready"], 1)
                link(V.reduce_sum(e, pr, AX.X))
            else:
                link(V.tensor_tensor(e, rows[:, :, :, D + 1], vals[L][:, t0:t0 + m, D].unsqueeze(2).to_broadcast((P, m, k)), ALU.add))
                link(V.scalar_tensor_tensor(out=e, in0=e, scalar=SLOPE, in1=e, op0=ALU.mult, op1=ALU.max))
            link(V.tensor_tensor(e, e, r.pen[:, t0:t0 + m, 0:k], ALU.add))
            mx = r.mx[:, 0:m]
            link(V.reduce_max(mx, e, AX.X))
            V.tensor_tensor(e, e, mx.unsqueeze(2).to_broadcast((P, m, k)), ALU.subtract).then_inc(f["scores_ready"], 1)

        def chunk_sum(L, at_):
            c = ORDER[L][at_]
            t0, m, k = CHUNKS[c]
            if k:
                neighbour_sum(L, c, TURN[L][at_])
                V.memset(r.used_mark[:], 0.0).then_inc(f["rows_used"], 1)
            if c >= NC - 2:
                no_neighbours(L, range(t0, t0 + m))

        def neighbour_sum(L, c, g):
            t0, m, k = CHUNKS[c]
            m = len(chunk_tiles(c))
            w = ROW if L else ROW0
            rows = gat[g % RING][:, 0:m * k * w].rearrange("p (t k w) -> p t k w", t=m, k=k)
            ef = r.e[g % 2]
            e = ef[:, 0:m * k].rearrange("p (t k) -> p t k", k=k)
            scored[0] += 1
            eng.wait_ge(f["exp_ready"], scored[0])
            link(V.reduce_sum(r.mx[:, 0:m], e, AX.X))
            link(V.reciprocal(r.mx[:, 0:m], r.mx[:, 0:m]))
            if t0 + m > ZERO_T:
                link(V.tensor_tensor(r.mx[:, 0:m], r.mx[:, 0:m], r.has[:, t0:t0 + m], ALU.mult))
            link(V.tensor_tensor(e, e, r.mx[:, 0:m].unsqueeze(2).to_broadcast((P, m, k)), ALU.mult))
            if m == 1:
                sums = (xp[:, t0, :], prod[:, 0:D])
                done = []
                for s in range(k):
                    if s >= 2:
                        eng.wait_ge(f["vector_step"], done[s - 2])
                    if s == 1:
                        ins = V.tensor_scalar(sums[1], rows[:, 0, s, 0:D], ef[:, s:s + 1], None, ALU.mult)
                    else:
                        ins = V.scalar_tensor_tensor(out=sums[s % 2], in0=rows[:, 0, s, 0:D], scalar=ef[:, s:s + 1],
                                                     in1=sums[s % 2], op0=ALU.mult, op1=ALU.add)
                    n[0] += 1
                    ins.then_inc(f["vector_step"], 1)
                    done.append(n[0])
                eng.wait_ge(f["vector_step"], n[0])
                link(V.tensor_tensor(sums[0], sums[0], sums[1], ALU.add))
                return
            for s in range(k):
                for i in range(m):
                    last = V.scalar_tensor_tensor(out=xp[:, t0 + i, :], in0=rows[:, i, s, 0:D], scalar=ef[:, i * k + s:i * k + s + 1],
                                                  in1=xp[:, t0 + i, :], op0=ALU.mult, op1=ALU.add)
                if s < k - 1:
                    link(last)
            link(last)

        def no_neighbours(L, tiles):
            if L == 1:
                eng.wait_ge(f["dense_used"], T)
                for t in tiles:
                    last = V.reciprocal(r.zr[:, t - ZERO_T:t - ZERO_T + 1], dense_out(t)[:, 0:1])
                link(last)
                zr = r.zr[:, tiles[0] - ZERO_T:tiles[-1] - ZERO_T + 1]
                link(V.tensor_tensor(zr, zr, r.empty[:, tiles[0]:tiles[-1] + 1], ALU.mult))
            else:
                eng.wait_ge(f["mean_ready"], 1 + (L + 1) // 2)
            for t in tiles:
                row, w = (dense_out(t)[:, 1:D + 1], r.zr[:, t - ZERO_T:t - ZERO_T + 1]) if L == 1 else (r.meanrow[:], r.empty[:, t:t + 1])
                last = V.scalar_tensor_tensor(out=xp[:, t, :], in0=row, scalar=w, in1=xp[:, t, :], op0=ALU.mult, op1=ALU.add)
            link(last)

        def dense(tiles):
            for j in tiles:
                eng.wait_ge(f["dense_added"], j + 1)
                b = db[j % DB][:, SKIP:]
                link(V.scalar_tensor_tensor(out=b, in0=b, scalar=SLOPE, in1=b, op0=ALU.mult, op1=ALU.max))
                V.scalar_tensor_tensor(out=b, in0=b, scalar=PENALTY[1], in1=m_row[:, SKIP:], op0=ALU.add, op1=ALU.subtract).then_inc(f["dense_shifted"], 1)

        scored = [0]
        for L in range(LAYERS):
            if L == 1:
                eng.wait_ge(f["projected_copied"], NG)
                link(V.reduce_max(r.dmax[:], vals[1][:, :, D + 1], AX.X))
                V.memset(r.scrap[:], 0.0).then_inc(f["target_max"], 1)
                for b in db:
                    last = V.memset(b[:, 0:SKIP], 1.0)
                eng.wait_ge(f["target_max_turned"], 1)
                link(V.reduce_max(r.dmax_one[:], r.ps[7][0:1, 0:P], AX.X))
                V.memset(r.scrap[:], 0.0).then_inc(f["target_max"], 1)
                eng.wait_ge(f["target_max_turned"], 2)
                link(V.tensor_copy(r.dmax_all[:], r.ps[7][:, P:P + 1]))
            for c in range(NC):
                if L == 1 and c == 0:
                    link(V.tensor_scalar(m_row, s_row, r.dmax_all[:, 0:1], None, ALU.add))
                    link(V.scalar_tensor_tensor(out=m_row, in0=m_row, scalar=SLOPE, in1=m_row, op0=ALU.mult, op1=ALU.max))
                    link(V.tensor_scalar(m_row, m_row, PENALTY[1], None, ALU.add))
                    dense(DENSE[0][:DENSE_FIRST])
                chunk_scores(L, c)
                if c and L < LAYERS - 1:
                    finish_norm(L + 1, c - 1)
                if L == 1 and c:
                    dense(DENSE[c][:DENSE_FIRST])
                chunk_sum(L, c)
                V.memset(r.scrap[:], 0.0).then_inc(f["chunk_done"], 1)
                if L < LAYERS - 1:
                    stats(ORDER[L][c])
                if L == 1:
                    dense(DENSE[c][DENSE_FIRST:])
            if L < LAYERS - 1:
                finish_norm(L + 1, NC - 1)

    def scalar(eng):
        S = nc.scalar
        eng.wait_ge(f["x_stats_ready"], 1)
        S.activation(r.std[:], r.mv[:, :, 1], ACT.Sqrt, bias=r.eps[:, 0:1]).then_inc(f["x_std_ready"], 1)
        eng.wait_ge(f["x_norm_ready"], 1)
        with eng.Fori(0, T // 6) as i:
            for u in range(6):
                def sign(s):
                    eng.wait_ge(f["adj_loaded%d%d" % (u % 3, s)], i * 32 + (16 * (u // 3) + 16))
                    S.activation(mask[u % 2][:, s, 0:SW], adjb[u % 3][:, s * SW:(s + 1) * SW], ACT.Sign, bias=r.minus_half[:, 0:1],
                                 accum_out=r.cnt[:, bass.ds(i * 6 + u, 1), s]).then_inc(f["mask_made"], 1)

                eng.wait_ge(f["mask_free"], i * 6 + (u + 1))
                sign(0)
                S.activation(r.query[:].rearrange("p (o d) -> p o d", o=1), rec[:, bass.ds(i * 6 + u, 1), 0:D], ACT.Relu, bias=r.shift[:, bass.ds(i * 6 + u, 1)],
                             scale=r.rstd[:, bass.ds(i * 6 + u, 1)]).then_inc(f["x_h_ready"], 1)
                sign(1)
                eng.wait_ge(f["x_turned"], i * 6 + (u + 1))
                S.copy(r.wa[:], r.ps[0][:, 0:D]).then_inc(f["x_turned_copied"], 1)
                sign(2)
                eng.wait_ge(f["x_projected"], i * 6 + (u + 1))
                S.copy(rec[:, bass.ds(i * 6 + u, 1), REC_Q:REC_Q + D], r.ps[2][:, 0:D].rearrange("p (o d) -> p o d", o=1)).then_inc(f["x_query_ready"], 1)

        def std(s, n):
            t0, m, k = CHUNKS[stage_order(s)[n]]
            eng.wait_ge(f["stats_ready"], (s - 1) * NC + n + 1)
            S.activation(r.std[:, t0:t0 + m], r.mv[:, t0:t0 + m, 1], ACT.Sqrt, bias=r.eps[:, 0:1]).then_inc(f["std_ready"], 1)

        def project(s, n):
            groups = chunk_groups(stage_order(s)[n])
            eng.wait_ge(f["norm_ready"], (s - 1) * NC + n + 1)
            for i in range(len(groups) + 2):
                if i < len(groups):
                    G = (s - 1) * NG + groups_before(s, n) + i
                    if G >= 2:
                        eng.wait_ge(f["turned"], G - 1)
                    for q, t in enumerate(groups[i]):
                        h = vals[1][:, t, 0:D] if s == 1 else hb[G % 2][:, q, :]
                        last = S.activation(h, xp[:, t, :], ACT.Relu, bias=r.shift[:, t:t + 1], scale=r.rstd[:, t:t + 1])
                    last.then_inc(f["h_ready"], 1)
                if 0 <= i - 1 < len(groups):
                    G = (s - 1) * NG + groups_before(s, n) + i - 1
                    w = len(groups[i - 1]) * D
                    eng.wait_ge(f["turned"], G + 1)
                    if G >= 2:
                        eng.wait_ge(f["projected"], G - 1)
                    S.copy(htb[G % 2][:, 0:w], r.ps[G % 2][:, 0:w]).then_inc(f["turned_copied"], 1)
                if s == 2 and n == NC - 2 and i == len(groups):
                    std(s, NC - 1)
                if 0 <= i - 2 < len(groups):
                    G = (s - 1) * NG + groups_before(s, n) + i - 2
                    ts = groups[i - 2]
                    eng.wait_ge(f["projected"], G + 1)
                    lo = D if s == 1 else 0
                    src = r.ps[2 + G % 2][:, 0:len(ts) * ROW].rearrange("p (t w) -> p t w", w=ROW)[:, :, lo:ROW]
                    dst = vals[s][:, ts[0]:ts[0] + len(ts), lo:ROW]
                    if s == 1 and ts[0] >= ZERO_T:
                        q = (ts[0] - ZERO_T) * P
                        S.copy(s_row[:, q:q + len(ts) * P], r.ps[5][:, 0:len(ts) * P])
                    S.copy(dst, src).then_inc(f["projected_copied"], 1)

        def mean(n, L):
            eng.wait_ge(f["mean_summed"], n)
            if n > 1:
                eng.wait_ge(f["chunk_done"], L * NC)
            S.mul(r.meanrow[:], r.ps[4][:, 0:D], 1.0 / N).then_inc(f["mean_ready"], 1)

        def dense_add(j):
            if j >= T:
                return
            if j >= DB:
                eng.wait_ge(f["dense_used"], j - DB + 1)
            S.activation(db[j % DB][:, SKIP:], s_row[:, SKIP:], ACT.Identity, bias=vals[1][:, j, D + 1:D + 2]).then_inc(f["dense_added"], 1)

        def dense_exp(j):
            eng.wait_ge(f["dense_shifted"], j + 1)
            S.activation(db[j % DB][:, SKIP:], db[j % DB][:, SKIP:], ACT.Exp).then_inc(f["dense_exp"], 1)

        scored = 0
        for L in range(LAYERS):
            if L != 1:
                mean(1 + (L + 1) // 2, L)
            for c in range(NC):
                g = TURN[L][c]
                def dense(i):
                    for j in DENSE[c][i:i + 1]:
                        dense_add(j + AHEAD)
                        dense_exp(j)

                def dense_first():
                    for i in range(DENSE_FIRST):
                        dense(i)

                if L == 1 and c == 0:
                    eng.wait_ge(f["projected_copied"], NG)
                    for j in range(AHEAD):
                        dense_add(j)
                    dense_first()
                m = GATHERS[ORDER[L][c]]
                if m:
                    scored += 1
                    eng.wait_ge(f["scores_ready"], scored)
                    S.activation(r.e[g % 2][:, 0:m], r.e[g % 2][:, 0:m], ACT.Exp, scale=SCALE[L]).then_inc(f["exp_ready"], 1)

                if L == 1 and c:
                    dense_first()
                if L < LAYERS - 1:
                    if c:
                        project(L + 1, c - 1)
                    if L != 1 or c not in (NC - 3, NC - 1):
                        std(L + 1, c)
                if L == 1:
                    for i in range(DENSE_FIRST, len(DENSE[c])):
                        dense(i)
                    if c == NC - 3:
                        std(L + 1, c)
            if L < LAYERS - 1:
                project(L + 1, NC - 1)

    def tensor(eng):
        M = nc.tensor
        eng.wait_ge(r.weights_ready, r.WEIGHTS_READY)
        with eng.Fori(0, T) as t:
            eng.wait_ge(f["x_h_ready"], t + 1)
            M.transpose(r.ps[0][:, 0:P], r.query[:], r.ident[:]).then_inc(f["x_turned"], 1)
            eng.wait_ge(f["x_turned_copied"], t + 1)
            M.matmul(r.ps[2][:, 0:D], r.wa[:], r.w0[:], start=True, stop=True).then_inc(f["x_projected"], 1)
        eng.wait_ge(f["tri_ready"], 1)
        eng.wait_ge(f["classes_ready"], 1)
        CT = CLASSES * T
        ind = r.ind[:, :, :].rearrange("p c t -> p (c t)")
        M.matmul(r.ps[1][:, 0:CT], r.ones_half[:], ind, start=True, stop=True)
        M.matmul(r.ps[0][:, 0:CT], r.tri[:], ind, start=True, stop=True).then_inc(f["ranks_ready"], 1)
        eng.wait_ge(f["bad_ready"], 1)
        M.matmul(r.ps[2][:, 0:1], r.ones[:], r.bad[:], start=True, stop=True).then_inc(f["bad_summed"], 1)

        def project(s, n):
            groups = chunk_groups(stage_order(s)[n])
            for i in range(len(groups) + 1):
                if i < len(groups):
                    G = (s - 1) * NG + groups_before(s, n) + i
                    eng.wait_ge(f["h_ready"], G + 1)
                    if G >= 2:
                        eng.wait_ge(f["turned_copied"], G - 1)
                    for q, t in enumerate(groups[i]):
                        h = vals[1][:, t, 0:D] if s == 1 else hb[G % 2][:, q, :]
                        last = M.transpose(r.ps[G % 2][:, q * P:(q + 1) * P], h, r.ident[:])
                    last.then_inc(f["turned"], 1)
                if i >= 1:
                    G = (s - 1) * NG + groups_before(s, n) + i - 1
                    ts = groups[i - 1]
                    eng.wait_ge(f["turned_copied"], G + 1)
                    if G >= 2:
                        eng.wait_ge(f["projected_copied"], G - 1)
                    if s == 1 and ts[0] >= ZERO_T:
                        if ts[0] > ZERO_T:
                            eng.wait_ge(f["projected_copied"], G)
                        M.matmul(r.ps[5][:, 0:len(ts) * P], r.source_rep[:], htb[G % 2][:, 0:len(ts) * P], start=True, stop=True)
                    lo = D if s == 1 else 0
                    for q, t in enumerate(ts):
                        last = M.matmul(r.ps[2 + G % 2][:, q * ROW + lo:(q + 1) * ROW], htb[G % 2][:, q * P:(q + 1) * P],
                                        r.wext[s][:, lo:ROW], start=True, stop=True)
                    last.then_inc(f["projected"], 1)

        for L in range(LAYERS):
            if L != 1:
                if L == 0:
                    eng.wait_ge(f["inp_loaded"], 16)
                else:
                    eng.wait_ge(f["projected_copied"], L * NG)
                v = inp if L == 0 else vals[L]
                if L == 2:
                    eng.wait_ge(f["chunk_done"], 2 * NC)
                for t in range(T):
                    last = M.matmul(r.ps[4][:, 0:D], r.ones[:], v[:, t, 0:D], start=(t == 0), stop=(t == T - 1))
                last.then_inc(f["mean_summed"], 1)
            if L == 1:
                eng.wait_ge(f["target_max"], 1)
                M.transpose(r.ps[7][0:1, 0:P], r.dmax[:], r.ident[:]).then_inc(f["target_max_turned"], 1)
                eng.wait_ge(f["target_max"], 2)
                M.matmul(r.ps[7][:, P:P + 1], r.ones[0:1, :], r.dmax_one[:], start=True, stop=True).then_inc(f["target_max_turned"], 1)
            for c in range(NC):

                def dense(i):
                    for j in DENSE[c][i:i + 1]:
                        eng.wait_ge(f["dense_exp"], j + 1)
                        if j == 0:
                            eng.wait_ge(f["mean_ready"], 1)
                            for b in range(4, 7):
                                M.matmul(r.ps[b][:, :], r.zeros[:], db[0][:, 0:BANK], start=True, stop=False, skip_group_check=True)
                        for t in range(ZERO_T, T):
                            q = (t - ZERO_T) * P
                            last = M.matmul(dense_out(t), db[j % DB][:, q:q + P], v_odd1[:, j, 0:D + 1], start=False, stop=(j == T - 1), skip_group_check=True)
                        last.then_inc(f["dense_used"], 1)

                if L == 1:
                    for i in range(DENSE_FIRST):
                        dense(i)
                if L < LAYERS - 1 and c:
                    project(L + 1, c - 1)
                if L == 1:
                    for i in range(DENSE_FIRST, len(DENSE[c])):
                        dense(i)
            if L < LAYERS - 1:
                project(L + 1, NC - 1)

    return sp, gpsimd, vector, scalar, tensor
class Names:
    pass


def semaphores(nc, ctx, prefix, names):
    return {name: ctx.enter_context(nc.semaphore(prefix + name)) for name in names.split()}


def setup(nc, r, w0_d, attn_d, w2_d, a2_d, w3_d, a3_d):

    def sp(eng):
        eng.dma_start(r.w0[:], w0_d).then_inc(r.weights_loaded, 16)
        for k in range(2):
            eng.dma_start(r.wext[1][:, D + k:D + k + 1], attn_d[k * D:(k + 1) * D, :]).then_inc(r.weights_loaded, 16)
        for L, w, a in ((2, w2_d, a2_d), (3, w3_d, a3_d)):
            eng.dma_start(r.wext[L][:, 0:D], w).then_inc(r.weights_loaded, 16)
            eng.dma_start(r.arow[L][:], a.rearrange("n o -> (o n)").partition_broadcast(P)).then_inc(r.weights_loaded, 16)

    def gpsimd(eng):
        eng.memset(r.ident[:], 0.0).then_inc(r.ident_ready, 1)
        eng.wait_ge(r.ident_ready, 1)
        eng.affine_select(out=r.ident[:], in_=r.ident[:], compare_op=ALU.not_equal, fill=1.0, base=0,
                          pattern=[[-1, P]], channel_multiplier=1).then_inc(r.weights_ready, 1)

    def vector(eng):
        nc.vector.memset(r.eps[:], EPS).then_inc(r.eps_ready, 1)
        eng.wait_ge(r.weights_loaded, 16 * 7)
        n = 0
        for L in (2, 3):
            for k in range(2):
                nc.vector.tensor_tensor(r.wa[:], r.wext[L][:, 0:D], r.arow[L][:, k * D:(k + 1) * D], ALU.mult).then_inc(r.setup_step, 1)
                n += 1
                eng.wait_ge(r.setup_step, n)
                nc.vector.reduce_sum(r.wext[L][:, D + k:D + k + 1], r.wa[:], AX.X).then_inc(r.setup_step, 1)
                n += 1
                eng.wait_ge(r.setup_step, n)
        for L in (1, 2, 3):
            last = nc.vector.tensor_copy(r.target_rep[L][:], r.wext[L][:, D + 1:D + 2].to_broadcast((P, P)))
            last.then_inc(r.weights_ready, 1)
        nc.vector.tensor_copy(r.source_rep[:], r.wext[1][:, D:D + 1].to_broadcast((P, P))).then_inc(r.weights_ready, 1)
        for i in range(CLASSES - 1):
            nc.vector.memset(r.caps[:, i:i + 1], float(SLOT_TILES[CLASSES - 2 - i] * P))
        nc.vector.memset(r.onesrow[:], 1.0)

    return sp, gpsimd, vector


def gnn_kernel(nc, x, adj, inp, w0, attn, w2, a2, w3, a3, out):
    ctx = ExitStack()
    with ctx:
        def sb(name, shape, dt=F32):
            return ctx.enter_context(nc.sbuf_tensor(name, shape, dt))

        def dram(name, shape):
            return nc.dram_tensor(name, shape, F32, kind="Internal").ap()

        r = Names()
        r.weights_loaded, r.weights_ready, r.ident_ready, r.eps_ready, r.setup_step = (
            ctx.enter_context(nc.semaphore(n)) for n in ("weights_loaded", "weights_ready", "ident_ready", "eps_ready", "setup_step"))
        r.arena = sb("arena", [P, ARENA])
        r.region = [r.arena[:, i * N:(i + 1) * N] for i in range(7)]
        r.ps = [ctx.enter_context(nc.psum_tensor(f"ps{i}", [P, BANK], F32)) for i in range(8)]
        r.w0 = sb("w0", [P, D])
        r.wext = [None] + [sb(f"wext{L}", [P, D + 2]) for L in (1, 2, 3)]
        r.arow = [None, None] + [sb(f"arow{L}", [P, 2 * D]) for L in (2, 3)]
        r.target_rep = [None] + [sb(f"target_rep{L}", [P, P]) for L in (1, 2, 3)]
        r.wa, r.ident, r.query, r.agg = (sb(n, [P, P]) for n in ("wa", "ident", "query", "agg"))
        r.eps, r.scrap, r.used_mark, r.rowmax, r.negmax, r.z, r.rz = (sb(n, [P, 1]) for n in ("eps", "scrap", "used_mark", "rowmax", "negmax", "z", "rz"))
        r.mean, r.var, r.std, r.rstd = (sb(n, [P, T]) for n in ("mean", "var", "std", "rstd"))
        r.score = sb("score", [P, T, 2])
        r.WEIGHTS_READY = 5
        r.ones, r.zeros, r.source_rep = (sb(n, [P, P]) for n in ("ones", "zeros", "source_rep"))
        r.tri, r.ones_half = (sb(n, [P, P], BF16) for n in ("tri", "ones_half"))
        r.zr, r.dmax_one = sb("zr", [P, ZT]), sb("dmax_one", [1, 1])
        r.minus_half, r.dmax, r.dmax_all, r.bad = (sb(n, [P, 1]) for n in ("minus_half", "dmax", "dmax_all", "bad"))
        r.bad2 = sb("bad2", [P, 2])
        r.ones_needle = sb("ones_needle", [P, FOUND], BF16)
        r.seg_base, r.number, r.number2 = (sb(n, [P, 2, SEG * FOUND]) for n in ("seg_base", "number", "number2"))
        r.found = sb("found", [P, 2, SEG * FOUND], U32)
        r.best = sb("best", [P, 2, 2 * FOUND])
        r.cnt = sb("cnt", [P, T, SEG])
        r.deg, r.posf, r.has, r.empty, r.shift = (sb(n, [P, T]) for n in ("deg", "posf", "has", "empty", "shift"))
        r.own_id, r.posi, r.low, r.high, r.place, r.own_p = (sb(n, [P, T], I32) for n in ("own_id", "posi", "low", "high", "place", "own_p"))
        r.ind = sb("ind", [P, CLASSES, T], BF16)
        r.rank, r.onesrow = (sb(n, [P, CLASSES * T]) for n in ("rank", "onesrow"))
        r.cum = sb("cum", [P, CLASSES * T + 1])
        r.seg_mark = sb("seg_mark", [P, 2 * SEG])
        r.caps, r.over = (sb(n, [P, CLASSES]) for n in ("caps", "over"))
        r.flag = sb("flag", [P, 1], I32)
        r.index0, r.index = (sb(n, [P, T, SLOTS], I32) for n in ("index0", "index"))
        r.pen = sb("pen", [P, T, SLOTS])
        r.bn = sb("bn", [P, T, 6])
        r.mv = sb("mv", [P, T, 2])
        r.e = [sb(f"e{i}", [P, CAP]) for i in range(2)]
        r.mx = sb("mx", [P, 16])
        r.dense_more = sb("dense_more", [P, ZT * P])
        r.meanrow = r.agg
        names = ("adj_loaded00 adj_loaded01 adj_loaded02 adj_loaded10 adj_loaded11 adj_loaded12 adj_loaded20 "
                 "adj_loaded21 adj_loaded22 bad_ready bad_summed chunk_done classes_ready dense_added "
                 "dense_exp dense_shifted dense_used exp_ready flag_ready gathered0 gathered1 "
                 "gathered2 h_ready id_ready index_ready inp_loaded mask_free mask_made "
                 "mean_ready mean_summed norm_ready place_ready places_ready pool_step projected "
                 "projected_copied ranks_ready rec_loaded0 rec_loaded1 rec_loaded2 rec_loaded3 rec_loaded4 "
                 "rec_scattered rows_used scores_ready search_step stats_ready std_ready stored "
                 "table0_written table_written target_max target_max_turned tri_ready turned turned_copied "
                 "vector_step x_h_ready x_loaded x_norm_ready x_projected x_query_ready x_stats_ready "
                 "x_std_ready x_turned x_turned_copied ")
        r.fast = semaphores(nc, ctx, "f_", names)
        rec_d = dram("records", (N, REC))
        tab_d = [dram(f"table{L}", (N, ROW if L else ROW0)) for L in range(LAYERS)]
        r.general = semaphores(nc, ctx, "g_", "x_loaded adj_loaded penalty_ready row_done stored vector_step var_ready std_ready h_ready "
                               "psum_filled psum_emptied query_ready score_filled scores_ready masked probs_ready probs_turned turned_copied aggregated")
        setup_sp, setup_pool, setup_dve = setup(nc, r, w0, attn, w2, a2, w3, a3)
        g_sp, g_dve, g_act, g_pe = general_path(nc, r, adj, x, inp, out)
        f_sp, f_pool, f_dve, f_act, f_pe = fast_path(nc, r, adj, x, inp, out, rec_d, tab_d)
        block = ctx.enter_context(nc.Block())

        def otherwise(eng, program):
            eng.wait_ge(r.fast["stored"], 16 * T)
            no_room = eng.value_load(r.flag[0:1, 0:1])
            with eng.If(no_room > 0):
                program(eng)

        @block.sync
        def _(sp):
            setup_sp(sp)
            f_sp(sp)
            otherwise(sp, g_sp)

        @block.gpsimd
        def _(pool):
            setup_pool(pool)
            f_pool(pool)

        @block.vector
        def _(dve):
            setup_dve(dve)
            f_dve(dve)
            otherwise(dve, g_dve)

        @block.scalar
        def _(act):
            act.wait_ge(r.eps_ready, 1)
            f_act(act)
            otherwise(act, g_act)

        @block.tensor
        def _(pe):
            f_pe(pe)
            otherwise(pe, g_pe)


_INS = ["x", "adj", "L0_gnn_input", "L0_gnn_weight", "L1_gnn_attn", "L2_gnn_W", "L2_gnn_a", "L3_gnn_Ws", "L3_gnn_a"]


def kernel(**inputs):
    import numpy as _np
    import concourse.bacc as _bacc
    from concourse import mybir as _mybir
    from concourse.bass_utils import run_bass_kernel_spmd as _run

    nc = _bacc.Bacc("TRN2", target_bir_lowering=False, num_devices=1)
    arrays, args = {}, []
    for name in _INS:
        a = _np.ascontiguousarray(inputs[name])
        arrays[f"in_{name}"] = a
        args.append(nc.dram_tensor(f"in_{name}", a.shape, _mybir.dt.from_np(a.dtype), kind="ExternalInput").ap())
    args.append(nc.dram_tensor("out_x", (N, D), _mybir.dt.float32, kind="ExternalOutput").ap())
    gnn_kernel(nc, *args)
    r = _run(nc, [arrays], core_ids=[0])
    return r.results[0]["out_x"]
```
